# Optimizing a Trainium2 kernel written in Bass

```python
import numpy as np
import jax
import jax.numpy as jnp

def _softmax(x, axis=-1):
    return jax.nn.softmax(x, axis=axis)

def _gelu(x):
    return jax.nn.gelu(x, approximate=True)

def _silu(x):
    return jax.nn.silu(x)

def _sigmoid(x):
    return jax.nn.sigmoid(x)

def _layernorm(x, axis=-1, eps=1e-05):
    m = jnp.mean(x, axis=axis, keepdims=True)
    v = jnp.var(x, axis=axis, keepdims=True)
    return (x - m) / jnp.sqrt(v + eps)

def _scatter_add(tgt, idx, src, axis=0):
    return tgt.at[idx].add(src)

def _segment_sum(src, seg, n):
    return jax.ops.segment_sum(src, seg, n)
kernel_name = 'mk_xattn_ffn_d1_seqx_r8_38d9ca'

def setup_inputs(seed: int=0):
    np.random.seed(seed)
    _w = jnp.asarray

    def _rec_inputs():
        import jax
        import jax.numpy as jnp
        _rk = jax.random.key(seed)
        x = -0.0003929 + 0.9999 * jax.random.normal(jax.random.fold_in(_rk, 1), (8, 256, 256), jnp.float32)
        _lenS = 256 - jax.random.randint(jax.random.fold_in(_rk, 7), (8,), 0, max(1, 256 // 4) + 1, jnp.int32)
        _lenS2 = 1601 - jax.random.randint(jax.random.fold_in(_rk, 8), (8,), 0, max(1, 1601 // 4) + 1, jnp.int32)
        _ctx_2048P = jax.random.normal(jax.random.fold_in(_rk, 11), (8, 16, 256), jnp.float32)
        _ctx_2048c = jax.random.dirichlet(jax.random.fold_in(_rk, 511), 0.3 * jnp.ones((16,), jnp.float32), (8, 1601))
        _ctx_2048t = jnp.einsum('bsk,bkd->bsd', _ctx_2048c, _ctx_2048P)
        _ctx_2048t = _ctx_2048t * jax.lax.rsqrt(jnp.mean(jnp.square(_ctx_2048t)) + 1e-12) * 0.953939
        ctx_2048 = -0.000514642 + 1.00011 * (_ctx_2048t + 0.3 * jax.random.normal(jax.random.fold_in(_rk, 611), (8, 1601, 256), jnp.float32))
        return (x, ctx_2048)
    x, ctx_2048 = _rec_inputs()

    def _L0_xattn_setup():
        import jax, jax.numpy as jnp
        import numpy as np
        FEAT = 256
        G = 16
        DG = FEAT // G
        key = jax.random.key(seed)
        ks = jax.random.split(key, 8)
        bs, N1, N2 = (2, 512, 64)
        s = 1.0 / np.sqrt(FEAT)
        return {'ref_feat': jax.random.normal(ks[0], (bs, N1, FEAT), jnp.float32), 'sup_feat': jax.random.normal(ks[1], (bs, N2, FEAT), jnp.float32), 'W_fc': jax.random.normal(ks[2], (FEAT, FEAT), jnp.float32) * s, 'b_fc': jnp.zeros((FEAT,), jnp.float32), 'W_q': jax.random.normal(ks[3], (FEAT, FEAT), jnp.float32) * s, 'b_q': jnp.zeros((FEAT,), jnp.float32), 'W_k': jax.random.normal(ks[4], (FEAT, FEAT), jnp.float32) * s, 'b_k': jnp.zeros((FEAT,), jnp.float32), 'W_v': jax.random.normal(ks[5], (FEAT, FEAT, 1, 1), jnp.float32) * 0.01, 'b_v': jnp.zeros((FEAT,), jnp.float32)}
    _L0_xattn_all = _L0_xattn_setup()
    _L0_xattn_in = {k: v for k, v in _L0_xattn_all.items() if k in ('W_fc', 'b_fc', 'W_q', 'b_q', 'W_k', 'b_k', 'W_v', 'b_v')}
    del _L0_xattn_all

    def _L0_ffn_setup():
        import jax, jax.numpy as jnp
        import numpy as np
        H, I, E, K = (256, 512, 8, 2)
        B, S = (1, 256)

        def _silu_mul(gu):
            d = gu.shape[-1] // 2
            return jax.nn.silu(gu[..., :d]) * gu[..., d:]
        key = jax.random.key(seed)
        ks = jax.random.split(key, 6)
        w_scale = 0.02
        return {'x': jax.random.normal(ks[0], (B, S, H), jnp.float32), 'gate_w': jax.random.normal(ks[1], (H, E), jnp.float32) * w_scale, 'base_gate_up': jax.random.normal(ks[2], (H, 2 * I), jnp.float32) * w_scale, 'base_down': jax.random.normal(ks[3], (I, H), jnp.float32) * w_scale, 'expert_gate_up': jax.random.normal(ks[4], (E, H, 2 * I), jnp.float32) * w_scale, 'expert_down': jax.random.normal(ks[5], (E, I, H), jnp.float32) * w_scale}
    _L0_ffn_all = _L0_ffn_setup()
    _L0_ffn_in = {k: v for k, v in _L0_ffn_all.items() if k in ('gate_w', 'base_gate_up', 'base_down', 'expert_gate_up', 'expert_down')}
    del _L0_ffn_all
    return {'x': x, 'ctx_2048': ctx_2048, 'L0_xattn_W_fc': _L0_xattn_in['W_fc'], 'L0_xattn_b_fc': _L0_xattn_in['b_fc'], 'L0_xattn_W_q': _L0_xattn_in['W_q'], 'L0_xattn_b_q': _L0_xattn_in['b_q'], 'L0_xattn_W_k': _L0_xattn_in['W_k'], 'L0_xattn_b_k': _L0_xattn_in['b_k'], 'L0_xattn_W_v': _L0_xattn_in['W_v'], 'L0_xattn_b_v': _L0_xattn_in['b_v'], 'L0_ffn_gate_w': _L0_ffn_in['gate_w'], 'L0_ffn_base_gate_up': _L0_ffn_in['base_gate_up'], 'L0_ffn_base_down': _L0_ffn_in['base_down'], 'L0_ffn_expert_gate_up': _L0_ffn_in['expert_gate_up'], 'L0_ffn_expert_down': _L0_ffn_in['expert_down']}

def reference(x, ctx_2048, L0_xattn_W_fc, L0_xattn_b_fc, L0_xattn_W_q, L0_xattn_b_q, L0_xattn_W_k, L0_xattn_b_k, L0_xattn_W_v, L0_xattn_b_v, L0_ffn_gate_w, L0_ffn_base_gate_up, L0_ffn_base_down, L0_ffn_expert_gate_up, L0_ffn_expert_down):
    import jax
    import jax.numpy as jnp

    def _L0_xattn_ref(ref_feat, sup_feat, W_fc, b_fc, W_q, b_q, W_k, b_k, W_v, b_v):
        import jax, jax.numpy as jnp
        import numpy as np
        FEAT = 256
        G = 16
        DG = FEAT // G
        bs, N1, _ = ref_feat.shape
        sup = jax.nn.relu(sup_feat @ W_fc.T + b_fc)
        ref = jax.nn.relu(ref_feat @ W_fc.T + b_fc)
        q = (ref @ W_q.T + b_q).reshape(bs, N1, G, DG)
        k = (sup @ W_k.T + b_k).reshape(bs, -1, G, DG)
        aff = jnp.einsum('bqhd,bkhd->bhqk', q, k) * (1.0 / np.sqrt(DG))
        p = jax.nn.softmax(aff, axis=-1)
        out_h = jnp.einsum('bhqk,bkf->bhqf', p, sup)
        Wv = W_v.reshape(G, DG, FEAT)
        attn = jnp.einsum('bhqf,hjf->bqhj', out_h, Wv).reshape(bs, N1, FEAT) + b_v
        return ref + attn

    def _L0_ffn_ref(x, gate_w, base_gate_up, base_down, expert_gate_up, expert_down):
        import jax, jax.numpy as jnp
        import numpy as np
        H, I, E, K = (256, 512, 8, 2)
        B, S = (1, 256)

        def _silu_mul(gu):
            d = gu.shape[-1] // 2
            return jax.nn.silu(gu[..., :d]) * gu[..., d:]
        base_y = _silu_mul(x @ base_gate_up) @ base_down
        b, s, h = x.shape
        xf = x.reshape(-1, h)
        n = xf.shape[0]
        n_exp = gate_w.shape[1]
        probs = jax.nn.softmax((xf @ gate_w).astype(jnp.float32), axis=-1)
        w, idx = jax.lax.top_k(probs, K)
        w = (w / w.sum(axis=-1, keepdims=True)).astype(x.dtype)
        comb = jnp.zeros((n, n_exp), x.dtype).at[jnp.arange(n)[:, None], idx].add(w)
        out = jnp.zeros_like(xf)
        for e in range(n_exp):
            y = _silu_mul(xf @ expert_gate_up[e]) @ expert_down[e]
            out = out + comb[:, e:e + 1] * y
        return out.reshape(b, s, h) + base_y
    x = x + _L0_xattn_ref(_layernorm(x, axis=-1), ctx_2048, L0_xattn_W_fc, L0_xattn_b_fc, L0_xattn_W_q, L0_xattn_b_q, L0_xattn_W_k, L0_xattn_b_k, L0_xattn_W_v, L0_xattn_b_v)
    x = x + _L0_ffn_ref(_layernorm(x, axis=-1), L0_ffn_gate_w, L0_ffn_base_gate_up, L0_ffn_base_down, L0_ffn_expert_gate_up, L0_ffn_expert_down)
    return x

_drawn_inputs = setup_inputs


def setup_inputs(seed=0):
    import zlib

    import numpy as np

    out = dict(_drawn_inputs(seed))
    spreads = {'L0_xattn_b_fc': (0.0, 0.1),
     'L0_xattn_b_q': (0.0, 0.8),
     'L0_xattn_b_k': (0.0, 0.8),
     'L0_xattn_b_v': (0.0, 0.1)}
    factors = {'L0_xattn_W_q': 8.0,
     'L0_xattn_W_k': 8.0,
     'L0_ffn_gate_w': 4.73,
     'L0_ffn_base_gate_up': 2.917,
     'L0_ffn_base_down': 2.918,
     'L0_ffn_expert_gate_up': 4.088,
     'L0_ffn_expert_down': 4.101}
    for name, (base, spread) in spreads.items():
        noise = np.random.default_rng([zlib.crc32(name.encode()), seed]).standard_normal(out[name].shape)
        drawn = base * np.exp(spread * noise) if base else spread * noise
        out[name] = jnp.asarray(drawn.astype(out[name].dtype))
    for name, factor in factors.items():
        out[name] = (out[name] * factor).astype(out[name].dtype)
    return out
```

```python
from contextlib import ExitStack

import concourse.bass as bass
from concourse import mybir

F32 = mybir.dt.float32
F32R = mybir.dt.float32r
ALU = mybir.AluOpType
ACT = mybir.ActivationFunctionType
AX = mybir.AxisListType

P = 128
B = 8
NQ = 256
NK = 1601
D = 256
KC = D // P
H = 16
DH = D // H
PAIRS = H // 2
EPS = 1e-5
QT = NQ // P
KT = -(-NK // P)
VS = DH + 1
VW = H * VS + 32 - VS

CHUNKS = [(0, NQ)] + [(o, 256) for o in range(0, NK - 65, 256)] + [(NK - 66, 66)]
NCH = len(CHUNKS)
RANGES = [(0, 402), (402, 400), (802, 400), (NK - 400, 400)]
HQ = H * QT
GROUPS = 4
STEPS = GROUPS * KT


def side_order():
    chunk = [("turn", 0), ("fc", 0), ("resid", 0), ("fc", 1), ("proj", 0)]
    for c in range(2, NCH):
        chunk += [("fc", c), ("proj", c - 1), ("val", c - 1)]
    chunk += [("proj", NCH - 1), ("val", NCH - 1)]
    score = [("score", n) for n in range(len(RANGES) * HQ)]
    need = [next(c for c in range(1, NCH) if min(CHUNKS[c][0] + CHUNKS[c][1], NK) >= o + w) for o, w in RANGES]
    steps = [[] for _ in range(STEPS)]
    done, nc_, ns_ = {}, 0, 0
    for s in range(STEPS - 3):
        while nc_ < len(chunk) and nc_ <= s * 0.9:
            steps[s].append(chunk[nc_])
            done[chunk[nc_]] = s
            nc_ += 1
        left = STEPS - 4 - s
        quota = -(-(len(score) - ns_) // max(left, 1)) if s >= 10 else 0
        quota = min(quota, 4)
        for _ in range(quota):
            if ns_ < len(score) and s >= done.get(("proj", need[ns_ // HQ]), STEPS) + 3:
                steps[s].append(score[ns_])
                ns_ += 1
    assert nc_ == len(chunk) and ns_ == len(score), (nc_, ns_)
    steps[STEPS - 2].append(("turnmax", 0))
    return steps


SIDE = side_order()
UNITS = [u for step in SIDE for u in step]
NU = len(UNITS)
UNIT_AT = {u: n for n, u in enumerate(UNITS)}
assert NU % 2 == 0
FIRST_UNIT = [sum(len(x) for x in SIDE[:s]) for s in range(STEPS + 1)]

STACK_DMAS = {c: 24 if c == 0 else 12 for c in range(NCH)}
STACK_SUM = [16 * sum(STACK_DMAS[i] for i in range(c)) for c in range(NCH + 1)]


def key_tile(kt):
    k0 = kt * P
    c = min(1 + k0 // 256, NCH - 1)
    return c, k0 - CHUNKS[c][0], min(P, NK - k0)


def setup(nc, t, x, weights, w_q, b_v):
    with ExitStack() as tmp:
        wraw = tmp.enter_context(nc.sbuf_tensor("wraw", [P, 3, KC, D], F32))
        xall = tmp.enter_context(nc.sbuf_tensor("xall", [P, B * QT, D], F32))
        stats = tmp.enter_context(nc.sbuf_tensor("stats", [P, B * QT, 6], F32))
        mv = tmp.enter_context(nc.sbuf_tensor("mv", [P, B * QT, 2], F32))
        half = tmp.enter_context(nc.sbuf_tensor("half", [P, B * QT], F32))
        vare = tmp.enter_context(nc.sbuf_tensor("vare", [P, B * QT], F32))
        w_in = [tmp.enter_context(nc.semaphore(f"w_in{i}")) for i in range(3)]
        x_all_in = tmp.enter_context(nc.semaphore("x_all_in"))
        small_in = tmp.enter_context(nc.semaphore("small_in"))
        w_hi_done = tmp.enter_context(nc.semaphore("w_hi_done"))
        w_lo_done = tmp.enter_context(nc.semaphore("w_lo_done"))
        stats_done = tmp.enter_context(nc.semaphore("stats_done"))
        var_done = tmp.enter_context(nc.semaphore("var_done"))
        rstd_done = tmp.enter_context(nc.semaphore("rstd_done"))
        set_done = tmp.enter_context(nc.semaphore("set_done"))
        ones_done = tmp.enter_context(nc.semaphore("ones_done"))
        with nc.Block() as block:

            @block.sync
            def _(sp):
                sp.dma_start(xall[:, :, :], x.rearrange("b (t p) d -> p (b t) d", p=P)).then_inc(x_all_in, 16)
                for i, w in enumerate(weights):
                    sp.dma_start(wraw[:, i, :, :], w.rearrange("(c p) n -> p c n", p=P)).then_inc(w_in[i], 16)
                for i, bias in enumerate(t.bias_in):
                    sp.dma_start(t.bias[:, i, :], bias.rearrange("(c p) -> p c", p=P),
                                 allow_slow_non_contiguous=True).then_inc(small_in, 16)
                sp.dma_start(t.bv[:, :], b_v.partition_broadcast(P)).then_inc(small_in, 16)
                sp.dma_start(t.wq[:, :, :], w_q.rearrange("(c p) n -> p c n", p=P)).then_inc(small_in, 16)
                sp.wait_ge(small_in, 16 * (len(t.bias_in) + 2))

            @block.gpsimd
            def _(pool):
                pool.memset(t.ident[:, :], 0.0).then_inc(set_done, 1)
                pool.memset(half[:, :], -0.5).then_inc(set_done, 1)
                pool.wait_ge(set_done, 1)
                pool.affine_select(out=t.ident[:, :], in_=t.ident[:, :], compare_op=ALU.not_equal, fill=1.0,
                                   base=0, pattern=[[-1, P]], channel_multiplier=1).then_inc(set_done, 1)
                for par in range(2):
                    pool.wait_ge(set_done, 3 + 3 * par)
                    pool.memset(t.qst[par][:, :, :].bitcast(F32), 0.0).then_inc(set_done, 1)
                    pool.wait_ge(set_done, 4 + 3 * par)
                    pool.memset(t.kst[par][96:97, :, :].bitcast(F32), 1.0).then_inc(set_done, 1)
                    pool.wait_ge(set_done, 5 + 3 * par)
                    pool.memset(t.v[par][:, :, :], 1.0).then_inc(set_done, 1)
                pool.wait_ge(var_done, 1)
                pool.wait_ge(set_done, 2)
                pool.tensor_tensor(t.rstd[:, :], vare[:, :], half[:, :], ALU.pow).then_inc(rstd_done, 1)
                pool.wait_ge(rstd_done, 1)
                pool.wait_ge(set_done, 9)

            @block.vector
            def _(dve):
                dve.wait_ge(x_all_in, 16)
                for i in range(B * QT):
                    dve.bn_stats(stats[:, i, :], xall[:, i, :]).then_inc(stats_done, 1)
                dve.wait_ge(stats_done, B * QT)
                for i in range(B * QT):
                    dve.bn_aggr(mv[:, i, :], stats[:, i, :]).then_inc(stats_done, 1)
                dve.wait_ge(stats_done, 2 * B * QT)
                dve.tensor_scalar(vare[:, :], mv[:, :, 1], EPS, None, ALU.add).then_inc(var_done, 1)
                dve.tensor_copy(t.mean[:, :], mv[:, :, 0]).then_inc(var_done, 1)
                for i in range(3):
                    dve.wait_ge(w_hi_done, i + 1)
                    dve.tensor_tensor(t.wlo[:, i, :, :], wraw[:, i, :, :], t.whi[:, i, :, :].bitcast(F32),
                                      ALU.subtract).then_inc(w_lo_done, 1)
                dve.wait_ge(w_lo_done, 3)
                dve.wait_ge(var_done, 2)

            @block.scalar
            def _(act):
                for i in range(3):
                    act.wait_ge(w_in[i], 16)
                    act.activation(t.whi[:, i, :, :], wraw[:, i, :, :], ACT.Copy).then_inc(w_hi_done, 1)


def attention(nc, t, x, ctx_t, x1):
    with ExitStack() as ctx:
        def sb(name, shape, dt):
            return ctx.enter_context(nc.sbuf_tensor(name, shape, dt))

        def sem(name):
            return ctx.enter_context(nc.semaphore(name))

        raw = sb("raw", [P, KC, 256], F32)
        chi = sb("chi", [P, KC, 256], F32R)
        clo = sb("clo", [P, KC, 256], F32R)
        fc = sb("fc", [P, KC, 256], F32)
        fhi = sb("fhi", [P, KC, 256], F32R)
        flo = sb("flo", [P, KC, 256], F32R)
        phi = sb("phi", [P, KC, 256], F32R)
        plo = sb("plo", [P, KC, 256], F32R)
        xn = fc
        res = [sb(f"res{i}", [P, QT, D], F32) for i in range(2)]
        prob = [sb(f"prob{i}", [P, 4 * NQ], F32) for i in range(2)]
        accsb = sb("accsb", [P, NQ], F32)
        att = accsb[:, 0:P].rearrange("p (q j d) -> p q j d", q=QT, d=DH)
        rec = sb("rec", [P, QT, 4], F32)
        mx = sb("mx", [P, HQ, len(RANGES)], F32)
        mxr = sb("mxr", [P, HQ], F32)
        mrow = sb("mrow", [HQ, P], F32R)
        st = [ctx.enter_context(nc.psum_tensor(f"st{i}", [P, 4 * NQ], F32)) for i in range(2)]
        acc = [ctx.enter_context(nc.psum_tensor(f"acc{i}", [P, 512], F32)) for i in range(2)]
        side = [ctx.enter_context(nc.psum_tensor(f"side{i}", [P, 512], F32)) for i in range(2)]

        side_full = sem("side_full")
        side_free = [sem("side_free0"), sem("side_free1")]
        raw_in = sem("raw_in")
        x_in = sem("x_in")
        xn_done = sem("xn_done")
        xb_done = sem("xb_done")
        hi_c = sem("hi_c")
        lo_c = sem("lo_c")
        hi_f = sem("hi_f")
        lo_f = sem("lo_f")
        phi_done = sem("phi_done")
        stack_in = sem("stack_in")
        row_in = sem("row_in")
        mx_done = sem("mx_done")
        st_full = sem("st_full")
        exp_done = sem("exp_done")
        pv_done = sem("pv_done")
        acc_out = sem("acc_out")
        ot_full = sem("ot_full")
        rec_done = sem("rec_done")
        norm_done = sem("norm_done")
        x1_ready = sem("x1_ready")
        x1_out = sem("x1_out")

        def after(eng, s, value, first):
            if not first:
                eng.wait_ge(s, value)

        def unit_full(eng, b, n):
            eng.wait_ge(side_full, b * NU + n + 1)

        def unit_out(eng, b, n):
            eng.wait_ge(side_free[n % 2], b * (NU // 2) + n // 2 + 1)

        def pe_unit(pe, b, par, n, first):
            kind, c = UNITS[n]
            bank = side[n % 2]
            after(pe, side_free[n % 2], b * (NU // 2) + n // 2, first and n < 2)
            if kind == "turn":
                pe.wait_ge(xn_done, QT * b + QT)
                for k in range(KC):
                    for q in range(QT):
                        mm = pe.transpose(bank[:, (k * QT + q) * P:(k * QT + q + 1) * P],
                                          xn[:, q, k * P:(k + 1) * P], t.ident[:, :])
            elif kind == "resid":
                unit_out(pe, b, UNIT_AT["fc", 0])
                for q in range(QT):
                    for k in range(KC):
                        mm = pe.transpose(bank[:, q * D + k * P:q * D + (k + 1) * P],
                                          fc[:, k, q * P:(q + 1) * P], t.ident[:, :])
            elif kind == "proj" and c == 0:
                for m in range(KC):
                    for k in range(KC):
                        mm = pe.matmul(bank[:, m * 256:m * 256 + NQ], t.wq[:, k, m * P:(m + 1) * P], fc[:, k, :],
                                       start=(k == 0), stop=(k == KC - 1))
            elif kind in ("fc", "proj"):
                w = CHUNKS[c][1]
                if kind == "fc":
                    pe.wait_ge(lo_c, NCH * b + c + 1)
                    wi, hi, lo = 0, chi, clo
                else:
                    pe.wait_ge(lo_f, (NCH - 1) * b + c)
                    wi, hi, lo = 1, fhi, flo
                for m in range(KC):
                    i = 0
                    for k in range(KC):
                        for wt, mov in ((t.whi, hi), (t.whi, lo), (t.wlo, hi)):
                            mm = pe.matmul(bank[:, m * 256:m * 256 + w], wt[:, wi, k, m * P:(m + 1) * P],
                                           mov[:, k, 0:w], start=(i == 0), stop=(i == 3 * KC - 1))
                            i += 1
            elif kind == "val":
                pe.wait_ge(lo_f, (NCH - 1) * b + c)
                tiles = [kt for kt in range(KT) if key_tile(kt)[0] == c]
                for j, kt in enumerate(tiles):
                    _, o, rows = key_tile(kt)
                    i = 0
                    for k in range(KC):
                        for a, wt in ((fhi, t.whi), (fhi, t.wlo), (flo, t.whi)):
                            mm = pe.matmul(bank[0:rows, j * D:(j + 1) * D], a[:, k, o:o + rows],
                                           wt[:, 2, k, :], start=(i == 0), stop=(i == 3 * KC - 1))
                            i += 1
            elif kind == "score":
                r, hq = divmod(c, HQ)
                if hq == 0:
                    o, w = RANGES[r]
                    last = next(i for i in range(1, NCH) if min(CHUNKS[i][0] + CHUNKS[i][1], NK) >= o + w)
                    pe.wait_ge(stack_in, b * STACK_SUM[NCH] + STACK_SUM[last + 1])
                o, w = RANGES[r]
                mm = pe.matmul(bank[:, 0:w], t.qst[par][0:96, hq // 4, (hq % 4) * P:(hq % 4 + 1) * P],
                               t.kst[par][0:96, hq // 4, o:o + w], start=True, stop=True)
            else:
                pe.wait_ge(mx_done, b + 1)
                mm = pe.transpose(bank[0:HQ, 0:P], mxr[:, :], t.ident[:, :])
            mm.then_inc(side_full, 1)

        def act_chunk_high(act, c):
            w = CHUNKS[c][1]
            act.activation(chi[:, :, 0:w], raw[:, :, 0:w], ACT.Copy).then_inc(hi_c, 1)

        def act_fc_high(act, b, c):
            w = CHUNKS[c][1]
            unit_out(act, b, UNIT_AT["fc", c])
            act.activation(fhi[:, :, 0:w], fc[:, :, 0:w], ACT.Copy).then_inc(hi_f, 1)

        def act_unit(act, b, par, n, first):
            kind, c = UNITS[n]
            bank = side[n % 2]
            if kind in ("resid", "score"):
                return
            unit_full(act, b, n)
            if kind == "turn":
                after(act, lo_c, NCH * b, first)
                act.activation(raw[:, :, :], bank[:, :].rearrange("p (k q) -> p k q", k=KC),
                               ACT.Copy).then_inc(side_free[n % 2], 1)
                unit_out(act, b, n)
                act_chunk_high(act, 0)
            elif kind == "fc":
                w = CHUNKS[c][1]
                if c == 1:
                    unit_full(act, b, UNIT_AT["proj", 0])
                else:
                    after(act, lo_f, (NCH - 1) * b + max(c - 1, 0), first and c == 0)
                for m in range(KC):
                    op = act.activation(fc[:, m, 0:w], bank[:, m * 256:m * 256 + w], ACT.Relu,
                                        bias=t.bias[:, 0, m:m + 1])
                op.then_inc(side_free[n % 2], 1)
                if c + 1 < NCH:
                    act.wait_ge(raw_in, 16 * ((NCH - 1) * b + c + 1))
                    act_chunk_high(act, c + 1)
                if c == 1:
                    act_fc_high(act, b, 1)
            elif kind == "proj":
                w = CHUNKS[c][1]
                after(act, stack_in, b * STACK_SUM[NCH] + STACK_SUM[c], first and c == 0)
                for m in range(KC):
                    op = act.activation(phi[:, m, 0:w], bank[:, m * 256:m * 256 + w], ACT.Identity,
                                        bias=t.bias[:, 1 if c == 0 else 2, m:m + 1])
                op.then_inc(phi_done, 1)
            elif kind == "val":
                tiles = [kt for kt in range(KT) if key_tile(kt)[0] == c]
                rows = key_tile(tiles[0])[2]
                k = len(tiles)
                dst = t.v[par][0:rows, tiles[0]:tiles[0] + k, 0:H * VS].rearrange("p k (h s) -> p k h s", s=VS)
                act.activation(dst[:, :, :, 0:DH],
                               bank[0:rows, 0:k * D].rearrange("p (k h s) -> p k h s", k=k, s=DH),
                               ACT.Copy).then_inc(side_free[n % 2], 1)
                if c + 1 < NCH:
                    act_fc_high(act, b, c + 1)
            else:
                after(act, row_in, 16 * b, first)
                act.activation(mrow[:, :], bank[0:HQ, 0:P], ACT.Copy, scale=-1.0).then_inc(side_free[n % 2], 1)

        def dve_unit(dve, b, par, n):
            kind, c = UNITS[n]
            bank = side[n % 2]
            if kind == "resid":
                unit_full(dve, b, n)
                dve.wait_ge(xb_done, b + 1)
                dve.tensor_tensor(res[par][:, :, :], bank[:, :].rearrange("p (q d) -> p q d", q=QT),
                                  res[par][:, :, :], ALU.add).then_inc(side_free[n % 2], 1)
            elif kind == "proj":
                w = CHUNKS[c][1]
                dve.wait_ge(phi_done, NCH * b + c + 1)
                for m in range(KC):
                    op = dve.scalar_tensor_tensor(plo[:, m, 0:w], in0=bank[:, m * 256:m * 256 + w],
                                                  scalar=t.bias[:, 1 if c == 0 else 2, m:m + 1],
                                                  in1=phi[:, m, 0:w].bitcast(F32), op0=ALU.add, op1=ALU.subtract)
                op.then_inc(side_free[n % 2], 1)
            elif kind == "score":
                r, hq = divmod(c, HQ)
                unit_full(dve, b, n)
                dve.tensor_reduce(mx[:, hq, r:r + 1], bank[:, 0:RANGES[r][1]], AX.X, ALU.max)\
                   .then_inc(side_free[n % 2], 1)
                if c == len(RANGES) * HQ - 1:
                    unit_out(dve, b, n)
                    unit_out(dve, b, n - 1)
                    dve.tensor_reduce(mxr[:, :], mx[:, :, :], AX.X, ALU.max).then_inc(mx_done, 1)

        def dve_normalise_input(dve, b, par):
            dve.wait_ge(x_in, 16 * (b + 1))
            for q in range(QT):
                mean, rstd = t.mean[:, bass.ds(QT * b + q, 1)], t.rstd[:, bass.ds(QT * b + q, 1)]
                dve.tensor_scalar(xn[:, q, :], res[par][:, q, :], mean, rstd, ALU.subtract, ALU.mult).then_inc(xn_done, 1)

        def pool_side(pool, b, par, first):
            def low_chunk(c):
                w = CHUNKS[c][1]
                pool.wait_ge(hi_c, NCH * b + c + 1)
                pool.tensor_tensor(clo[:, :, 0:w], raw[:, :, 0:w], chi[:, :, 0:w].bitcast(F32),
                                   ALU.subtract).then_inc(lo_c, 1)

            def low_fc(c):
                w = CHUNKS[c][1]
                pool.wait_ge(hi_f, (NCH - 1) * b + c)
                pool.tensor_tensor(flo[:, :, 0:w], fc[:, :, 0:w], fhi[:, :, 0:w].bitcast(F32),
                                   ALU.subtract).then_inc(lo_f, 1)

            pool.wait_ge(xn_done, QT * (b + 1))
            for q in range(QT):
                op = pool.tensor_tensor(res[par][:, q, :], res[par][:, q, :], t.bv[:, :], ALU.add)
            op.then_inc(xb_done, 1)
            low_chunk(0)
            for c in range(NCH):
                if c + 1 < NCH:
                    low_chunk(c + 1)
                if c > 0:
                    low_fc(c)

        def sp_load_x(sp, b, par, first):
            after(sp, x1_out, 16 * (b - 1), first)
            sp.dma_start(res[par][:, :, :], x[b].rearrange("(t p) d -> p t d", p=P)).then_inc(x_in, 16)

        def sp_side(sp, b, par):
            for c in range(1, NCH):
                o, w = CHUNKS[c]
                sp.wait_ge(lo_c, NCH * b + c)
                sp.dma_start(raw[:, :, 0:w], ctx_t[b].rearrange("(k p) n -> p k n", p=P)[:, :, o:o + w])\
                  .then_inc(raw_in, 16)
                if c >= 2:
                    sp_stack(sp, b, par, c - 2)
            sp_stack(sp, b, par, NCH - 2)
            sp_stack(sp, b, par, NCH - 1)
            unit_out(sp, b, UNIT_AT["turnmax", 0])
            sp.dma_start(t.qst[par][96:97, :, :].rearrange("p a n -> p (a n)").bitcast(F32),
                         mrow[:, :].bitcast(F32)).then_inc(row_in, 16)

        def sp_stack(sp, b, par, c):
            unit_out(sp, b, UNIT_AT["proj", c])
            for g in range(3):
                for p in range(4):
                    if c == 0:
                        part = (phi, phi, plo)[g]
                        for j in range(2):
                            dst = t.qst[par][32 * g + 16 * j:32 * g + 16 * j + 16, p::4, j * NQ:(j + 1) * NQ]
                            src = part[32 * p + 16 * j:32 * p + 16 * j + 16, :, 0:NQ]
                            sp.dma_start(dst.bitcast(F32), src.bitcast(F32)).then_inc(stack_in, 16)
                    else:
                        o, w = CHUNKS[c]
                        lead = max(CHUNKS[c - 1][0] + CHUNKS[c - 1][1] - o, 0) if c > 1 else 0
                        part = (phi, plo, phi)[g]
                        dst = t.kst[par][32 * g:32 * g + 32, p::4, o + lead:o + w]
                        src = part[32 * p:32 * p + 32, :, lead:w]
                        sp.dma_start(dst.bitcast(F32), src.bitcast(F32)).then_inc(stack_in, 16)

        def pe_scores(pe, b, par, s, first):
            g, kt = divmod(s, KT)
            rows = key_tile(kt)[2]
            if s == 0:
                pe.wait_ge(row_in, 16 * (b + 1))
            after(pe, exp_done, STEPS * b + s - 1, first and s < 2)
            for i in range(2):
                mm = pe.matmul(st[s % 2][0:rows, i * 2 * NQ:(i + 1) * 2 * NQ],
                               t.kst[par][0:97, 2 * g + i, kt * P:kt * P + rows],
                               t.qst[par][0:97, 2 * g + i, :], start=True, stop=True)
            mm.then_inc(st_full, 1)

        def pe_values(pe, b, par, s, first):
            g, kt = divmod(s, KT)
            rows = key_tile(kt)[2]
            pe.wait_ge(exp_done, STEPS * b + s + 1)
            if kt == 0:
                after(pe, norm_done, GROUPS * b + g - 1, first and g < 2)
            for j in range(4):
                h = 4 * g + j
                mm = pe.matmul(acc[g % 2][32 * j:32 * j + 32, 0:NQ], t.v[par][0:rows, kt, VS * h:VS * h + 32],
                               prob[s % 2][0:rows, j * NQ:(j + 1) * NQ], start=(kt == 0), stop=(kt == KT - 1))
            mm.then_inc(pv_done, 1)

        def pe_turn_out(pe, b, g):
            pe.wait_ge(acc_out, GROUPS * b + g + 1)
            for q in range(QT):
                mm = pe.transpose(acc[g % 2][:, NQ + q * P:NQ + (q + 1) * P], accsb[:, q * P:(q + 1) * P],
                                  t.ident[:, :])
            mm.then_inc(ot_full, 1)

        def dve_acc_out(dve, b, g, first):
            dve.wait_ge(pv_done, STEPS * b + KT * (g + 1))
            after(dve, ot_full, GROUPS * b + g, first and g == 0)
            after(dve, x1_ready, GROUPS * b + g, first and g == 0)
            dve.tensor_copy(accsb[:, :], acc[g % 2][:, 0:NQ]).then_inc(acc_out, 1)

        def dve_normalise(dve, b, par, g):
            dve.wait_ge(ot_full, GROUPS * b + g + 1)
            o = acc[g % 2][:, NQ:2 * NQ].rearrange("p (q j s) -> p q j s", q=QT, s=32)
            dve.reciprocal(rec[:, :, :], o[:, :, :, DH]).then_inc(rec_done, 1)
            dve.wait_ge(rec_done, GROUPS * b + g + 1)
            dve.tensor_tensor(att, o[:, :, :, 0:DH],
                              rec[:, :, :].unsqueeze(3).broadcast_to([P, QT, 4, DH]),
                              ALU.mult).then_inc(norm_done, 1)
            dve.wait_ge(norm_done, GROUPS * b + g + 1)
            r = res[par][:, :, g * 4 * DH:(g + 1) * 4 * DH]
            dve.tensor_tensor(r, r, att.rearrange("p q j s -> p q (j s)"), ALU.add)\
               .then_inc(x1_ready, 1)

        def sp_store(sp, b, par):
            sp.wait_ge(x1_ready, GROUPS * (b + 1))
            sp.dma_start(x1[b].rearrange("(t p) d -> p t d", p=P), res[par][:, :, :]).then_inc(x1_out, 16)

        def batches(eng, body):
            body(0, 0, True, False)
            with eng.Fori(0, B // 2 - 1) as i:
                body(2 * i + 1, 1, False, False)
                body(2 * i + 2, 0, False, False)
            body(B - 1, 1, False, True)

        with nc.Block() as block:

            @block.sync
            def _(sp):
                def body(b, par, first, last):
                    if not last:
                        sp_load_x(sp, b + 1, 1 - par, first)
                        sp_side(sp, b + 1, 1 - par)
                    sp_store(sp, b, par)

                sp_load_x(sp, 0, 0, True)
                sp_side(sp, 0, 0)
                batches(sp, body)
                sp.wait_ge(x1_out, 16 * B)

            @block.gpsimd
            def _(pool):
                pool_side(pool, 0, 0, True)
                with pool.Fori(0, B // 2 - 1) as i:
                    pool_side(pool, 2 * i + 1, 1, False)
                    pool_side(pool, 2 * i + 2, 0, False)
                pool_side(pool, B - 1, 1, False)

            @block.scalar
            def _(act):
                def body(b, par, first, last):
                    for s in range(STEPS):
                        rows = key_tile(s % KT)[2]
                        act.wait_ge(st_full, STEPS * b + s + 1)
                        if not (first and s < 2):
                            act.wait_ge(pv_done, STEPS * b + s - 1)
                        act.activation(prob[s % 2][0:rows, :], st[s % 2][0:rows, :], ACT.Exp,
                                       scale=float(DH) ** -0.5).then_inc(exp_done, 1)
                        if not last:
                            for n in range(FIRST_UNIT[s], FIRST_UNIT[s + 1]):
                                act_unit(act, b + 1, 1 - par, n, False)

                for n in range(NU):
                    act_unit(act, 0, 0, n, True)
                batches(act, body)

            @block.vector
            def _(dve):
                def body(b, par, first, last):
                    if not last:
                        dve_normalise_input(dve, b + 1, 1 - par)
                    for s in range(STEPS):
                        g, kt = divmod(s, KT)
                        if kt == 1 and g > 0:
                            dve_acc_out(dve, b, g - 1, first)
                        if kt == 3 and g > 0:
                            dve_normalise(dve, b, par, g - 1)
                        if not last:
                            for n in range(FIRST_UNIT[s], FIRST_UNIT[s + 1]):
                                dve_unit(dve, b + 1, 1 - par, n)
                    dve_acc_out(dve, b, GROUPS - 1, first)
                    dve_normalise(dve, b, par, GROUPS - 1)

                dve_normalise_input(dve, 0, 0)
                for n in range(NU):
                    dve_unit(dve, 0, 0, n)
                batches(dve, body)

            @block.tensor
            def _(pe):
                def body(b, par, first, last):
                    for s in range(STEPS):
                        g, kt = divmod(s, KT)
                        pe_scores(pe, b, par, s, first)
                        lo, hi = FIRST_UNIT[s], FIRST_UNIT[s + 1]
                        mid = (lo + hi) // 2
                        if not last:
                            for n in range(lo, mid):
                                pe_unit(pe, b + 1, 1 - par, n, False)
                        if s > 0:
                            pe_values(pe, b, par, s - 1, first)
                        if kt == 2 and g > 0:
                            pe_turn_out(pe, b, g - 1)
                        if not last:
                            for n in range(mid, hi):
                                pe_unit(pe, b + 1, 1 - par, n, False)
                    pe_values(pe, b, par, STEPS - 1, first)
                    pe_turn_out(pe, b, GROUPS - 1)

                for n in range(NU):
                    pe_unit(pe, 0, 0, n, True)
                batches(pe, body)


I = 512
E = 8
FT = I // P
T = B * NQ // P
TW = 512
TC = B * NQ // TW


def ffn(nc, ident, x1, gate_w, gate_up, down, out):
    with ExitStack() as ctx:
        def sb(name, shape, dt):
            return ctx.enter_context(nc.sbuf_tensor(name, shape, dt))

        def sem(name):
            return ctx.enter_context(nc.semaphore(name))

        y = sb("y", [P, T, D], F32)
        stats = sb("stats2", [P, T, 6], F32)
        mv = sb("mv2", [P, T, 2], F32)
        vare = sb("vare2", [P, T], F32)
        half = sb("half2", [P, T], F32)
        rstd = sb("rstd2", [P, T], F32)
        xn = sb("xn2", [P, 2, D], F32)
        xnt = sb("xnt", [P, KC, T * P], F32)
        gw = sb("gw", [P, KC, E], F32)
        lt = sb("lt", [E, T * P], F32)
        top = sb("top", [P, T], F32)
        ex = sb("ex", [P, T, E], F32)
        pr = sb("pr", [P, T, E], F32)
        beats = sb("beats", [P, T, E, E], F32)
        rank = sb("rank", [P, T, E], F32)
        comb = sb("comb", [P, T, E + 1], F32)
        wgu = [sb(f"wgu{i}", [P, KC, 2 * I], F32) for i in range(2)]
        wdn = [sb(f"wdn{i}", [P, FT, D], F32) for i in range(2)]
        sil = [sb(f"sil{i}", [P, TW], F32) for i in range(2)]
        h = [sb(f"h{i}", [P, FT, TW], F32) for i in range(2)]
        pg = [ctx.enter_context(nc.psum_tensor(f"pg{i}", [P, TW], F32)) for i in range(2)]
        pu = [ctx.enter_context(nc.psum_tensor(f"pu{i}", [P, TW], F32)) for i in range(2)]
        py = [ctx.enter_context(nc.psum_tensor(f"py{i}", [P, D], F32)) for i in range(4)]

        y_in = sem("y_in")
        gw_in = sem("gw_in")
        w_in = [sem("ew_in0"), sem("ew_in1")]
        out_done = sem("out_done")
        st_done = sem("st_done")
        v_done = sem("v_done")
        half_done = sem("half_done")
        r_done = sem("r_done")
        n_done = sem("n_done")
        turned = sem("turned")
        xnt_done = sem("xnt_done")
        logit_full = sem("logit_full")
        lt_done = sem("lt_done")
        lt_turned = sem("lt_turned")
        chain = sem("chain")
        sub_done = sem("sub_done")
        exp_done = sem("gate_exp_done")
        comb_done = sem("comb_done")
        g_full = sem("g_full")
        sil_done = sem("sil_done")
        h_done = sem("h_done")
        y_full = sem("y_full")
        y_done = sem("y_done")

        def after(eng, s, value, first):
            if not first:
                eng.wait_ge(s, value)

        def experts(eng, body):
            body(0, 0, True)
            body(1, 1, False)
            with eng.Fori(1, E // 2) as i:
                body(2 * i, 0, False)
                body(2 * i + 1, 1, False)
            body(E, 0, False)

        with nc.Block() as block:

            @block.sync
            def _(sp):
                sp.dma_start(y[:, :, :], x1.rearrange("b (t p) d -> p (b t) d", p=P)).then_inc(y_in, 16)
                sp.dma_start(gw[:, :, :], gate_w.rearrange("(k p) e -> p k e", p=P)).then_inc(gw_in, 16)

                def load(e, par, first):
                    after(sp, y_full, T * (e - 1), first)
                    sp.dma_start(wgu[par][:, :, :], gate_up[e].rearrange("(k p) n -> p k n", p=P))\
                      .then_inc(w_in[par], 16)
                    sp.dma_start(wdn[par][:, :, :], down[e].rearrange("(k p) n -> p k n", p=P))\
                      .then_inc(w_in[par], 16)

                load(0, 0, True)
                load(1, 1, True)
                with sp.Fori(1, E // 2) as i:
                    load(2 * i, 0, False)
                    load(2 * i + 1, 1, False)
                load(E, 0, False)
                sp.wait_ge(y_done, (E + 1) * T)
                sp.dma_start(out.rearrange("b (t p) d -> p (b t) d", p=P), y[:, :, :]).then_inc(out_done, 16)
                sp.wait_ge(out_done, 16)

            @block.gpsimd
            def _(pool):
                pool.memset(half[:, :], -0.5).then_inc(half_done, 1)
                pool.memset(comb[:, :, E:E + 1], 1.0).then_inc(half_done, 1)
                pool.wait_ge(half_done, 1)
                pool.wait_ge(v_done, 1)
                pool.tensor_tensor(rstd[:, :], vare[:, :], half[:, :], ALU.pow).then_inc(r_done, 1)

            @block.vector
            def _(dve):
                links = [0]

                def link(op):
                    links[0] += 1
                    op.then_inc(chain, 1)
                    dve.wait_ge(chain, links[0])

                dve.wait_ge(y_in, 16)
                for i in range(T):
                    dve.bn_stats(stats[:, i, :], y[:, i, :]).then_inc(st_done, 1)
                dve.wait_ge(st_done, T)
                for i in range(T):
                    dve.bn_aggr(mv[:, i, :], stats[:, i, :]).then_inc(st_done, 1)
                dve.wait_ge(st_done, 2 * T)
                dve.tensor_scalar(vare[:, :], mv[:, :, 1], EPS, None, ALU.add).then_inc(v_done, 1)
                dve.wait_ge(r_done, 1)
                for i in range(T):
                    if i >= 2:
                        dve.wait_ge(turned, i - 1)
                    dve.tensor_scalar(xn[:, i % 2, :], y[:, i, :], mv[:, i, 0:1], rstd[:, i:i + 1],
                                      ALU.subtract, ALU.mult).then_inc(n_done, 1)
                dve.wait_ge(lt_turned, 1)
                logits = pg[0][:, 0:T * E].rearrange("p (t e) -> p t e", e=E)
                link(dve.tensor_reduce(top[:, :], logits, AX.X, ALU.max))
                dve.tensor_tensor(ex[:, :, :], logits, top[:, :].unsqueeze(2).broadcast_to([P, T, E]),
                                  ALU.subtract).then_inc(sub_done, 1)
                dve.wait_ge(exp_done, 1)
                link(dve.tensor_reduce(top[:, :], ex[:, :, :], AX.X, ALU.add))
                link(dve.reciprocal(top[:, :], top[:, :]))
                link(dve.tensor_tensor(pr[:, :, :], ex[:, :, :], top[:, :].unsqueeze(2).broadcast_to([P, T, E]),
                                       ALU.mult))
                for e in range(E):
                    if e > 0:
                        dve.tensor_tensor(beats[:, :, e, 0:e], pr[:, :, e:e + 1].broadcast_to([P, T, e]),
                                          pr[:, :, 0:e], ALU.is_gt)
                    op = dve.tensor_tensor(beats[:, :, e, e:E], pr[:, :, e:e + 1].broadcast_to([P, T, E - e]),
                                           pr[:, :, e:E], ALU.is_ge)
                link(op)
                link(dve.tensor_reduce(rank[:, :, :], beats[:, :, :, :].rearrange("p t a b -> p t b a"), AX.X,
                                       ALU.add))
                link(dve.scalar_tensor_tensor(comb[:, :, 0:E], in0=rank[:, :, :], scalar=2.5, in1=pr[:, :, :],
                                              op0=ALU.is_lt, op1=ALU.mult))
                link(dve.tensor_reduce(top[:, :], comb[:, :, 0:E], AX.X, ALU.add))
                link(dve.reciprocal(top[:, :], top[:, :]))
                link(dve.tensor_tensor(comb[:, :, 0:E], comb[:, :, 0:E],
                                       top[:, :].unsqueeze(2).broadcast_to([P, T, E]), ALU.mult))
                dve.wait_ge(half_done, 2)

                def body(e, par, first):
                    for c in range(TC):
                        n = TC * e + c
                        for f in range(FT):
                            dve.wait_ge(sil_done, FT * n + f + 1)
                            if f == 0:
                                after(dve, y_full, 4 * (n - 1), first and c < 2)
                            dve.tensor_tensor(h[c % 2][:, f, :], sil[f % 2][:, :], pu[f % 2][:, :],
                                              ALU.mult).then_inc(h_done, 1)
                        for q in range(4):
                            t = 4 * c + q
                            dve.wait_ge(y_full, 4 * n + q + 1)
                            w = comb[:, t, :][:, bass.ds(e, 1)]
                            dve.scalar_tensor_tensor(y[:, t, :], in0=py[q][:, :], scalar=w, in1=y[:, t, :],
                                                     op0=ALU.mult, op1=ALU.add).then_inc(y_done, 1)

                experts(dve, body)

            @block.scalar
            def _(act):
                for i in range(T):
                    act.wait_ge(turned, i + 1)
                    act.activation(xnt[:, :, i * P:(i + 1) * P],
                                   py[i % 4][:, :].rearrange("p (k q) -> p k q", k=KC), ACT.Copy)\
                       .then_inc(xnt_done, 1)
                for c in range(TC):
                    act.wait_ge(logit_full, c + 1)
                    act.activation(lt[:, c * TW:(c + 1) * TW], pu[c % 2][0:E, :], ACT.Copy).then_inc(lt_done, 1)
                act.wait_ge(sub_done, 1)
                act.activation(ex[:, :, :], ex[:, :, :], ACT.Exp).then_inc(exp_done, 1)

                def body(e, par, first):
                    for c in range(TC):
                        n = TC * e + c
                        for f in range(FT):
                            act.wait_ge(g_full, FT * n + f + 1)
                            after(act, h_done, FT * n + f - 1, first and c == 0 and f < 2)
                            act.activation(sil[f % 2][:, :], pg[f % 2][:, :], ACT.Silu).then_inc(sil_done, 1)

                experts(act, body)

            @block.tensor
            def _(pe):
                for i in range(T):
                    pe.wait_ge(n_done, i + 1)
                    if i >= 4:
                        pe.wait_ge(xnt_done, i - 3)
                    for k in range(KC):
                        mm = pe.transpose(py[i % 4][:, k * P:(k + 1) * P], xn[:, i % 2, k * P:(k + 1) * P],
                                          ident[:, :])
                    mm.then_inc(turned, 1)
                pe.wait_ge(gw_in, 16)
                pe.wait_ge(xnt_done, T)
                for c in range(TC):
                    if c >= 2:
                        pe.wait_ge(lt_done, c - 1)
                    for k in range(KC):
                        mm = pe.matmul(pu[c % 2][0:E, :], gw[:, k, :], xnt[:, k, c * TW:(c + 1) * TW],
                                       start=(k == 0), stop=(k == KC - 1))
                    mm.then_inc(logit_full, 1)
                pe.wait_ge(lt_done, TC)
                for i in range(T):
                    mm = pe.transpose(pg[0][:, i * E:(i + 1) * E], lt[:, i * P:(i + 1) * P], ident[0:E, 0:E])
                mm.then_inc(lt_turned, 1)
                pe.wait_ge(sub_done, 1)

                def body(e, par, first):
                    pe.wait_ge(w_in[par], 16 * (e + 2 - par))
                    for c in range(TC):
                        n = TC * e + c
                        for f in range(FT):
                            after(pe, h_done, FT * n + f - 1, first and c == 0 and f < 2)
                            for dst, o in ((pg[f % 2], f * P), (pu[f % 2], I + f * P)):
                                for k in range(KC):
                                    mm = pe.matmul(dst[:, :], wgu[par][:, k, o:o + P],
                                                   xnt[:, k, c * TW:(c + 1) * TW], start=(k == 0),
                                                   stop=(k == KC - 1))
                            mm.then_inc(g_full, 1)
                        pe.wait_ge(h_done, FT * (n + 1))
                        for q in range(4):
                            after(pe, y_done, 4 * (n - 1) + q + 1, first and c == 0)
                            for f in range(FT):
                                mm = pe.matmul(py[q][:, :], h[c % 2][:, f, q * P:(q + 1) * P], wdn[par][:, f, :],
                                               start=(f == 0), stop=(f == FT - 1))
                            mm.then_inc(y_full, 1)

                experts(pe, body)


class Kept:
    pass


def attend(nc, x, ctx_t, w_fc, b_fc, w_q, b_q, w_k, b_k, w_v, b_v, x1, ident):
    with ExitStack() as ctx:
        def sb(name, shape, dt):
            return ctx.enter_context(nc.sbuf_tensor(name, shape, dt))

        t = Kept()
        t.kst = [sb(f"kst{i}", [P, PAIRS, NK], F32R) for i in range(2)]
        t.qst = [sb(f"qst{i}", [P, PAIRS, 2 * NQ], F32R) for i in range(2)]
        t.v = [sb(f"v{i}", [P, KT, VW], F32) for i in range(2)]
        t.whi = sb("whi", [P, 3, KC, D], F32R)
        t.wlo = sb("wlo", [P, 3, KC, D], F32R)
        t.wq = sb("wq", [P, KC, D], F32)
        t.bias = sb("bias", [P, 3, KC], F32)
        t.bias_in = [b_fc, b_q, b_k]
        t.bv = sb("bv", [P, D], F32)
        t.ident = ident
        t.mean = sb("mean", [P, B * QT], F32)
        t.rstd = sb("rstd", [P, B * QT], F32)
        setup(nc, t, x, [w_fc, w_k, w_v], w_q, b_v)
        attention(nc, t, x, ctx_t, x1)


def program(nc, x, ctx_t, w_fc, b_fc, w_q, b_q, w_k, b_k, w_v, b_v, gate_w, gate_up, down, out):
    x1 = nc.dram_tensor("x1", [B, NQ, D], F32).ap()
    with nc.sbuf_tensor("ident", [P, P], F32) as ident:
        attend(nc, x, ctx_t, w_fc, b_fc, w_q, b_q, w_k, b_k, w_v, b_v, x1, ident)
        ffn(nc, ident, x1, gate_w, gate_up, down, out)


def kernel(**inputs):
    import numpy as np
    import concourse.bacc as bacc
    from concourse.bass_utils import run_bass_kernel_spmd

    a = {n: np.asarray(v) for n, v in inputs.items()}
    arrays = {
        "x": a["x"],
        "ctx_t": np.ascontiguousarray(a["ctx_2048"].transpose(0, 2, 1)),
        "w_fc": np.ascontiguousarray(a["L0_xattn_W_fc"].T), "b_fc": a["L0_xattn_b_fc"],
        "w_q": np.ascontiguousarray(a["L0_xattn_W_q"].T), "b_q": a["L0_xattn_b_q"],
        "w_k": np.ascontiguousarray(a["L0_xattn_W_k"].T), "b_k": a["L0_xattn_b_k"],
        "w_v": np.ascontiguousarray(a["L0_xattn_W_v"].reshape(D, D).T), "b_v": a["L0_xattn_b_v"],
        "gate_w": a["L0_ffn_gate_w"],
        "gate_up": np.concatenate([a["L0_ffn_expert_gate_up"], a["L0_ffn_base_gate_up"][None]]),
        "down": np.concatenate([a["L0_ffn_expert_down"], a["L0_ffn_base_down"][None]]),
    }
    nc = bacc.Bacc("TRN2", target_bir_lowering=False, num_devices=1)
    ins = [nc.dram_tensor(n, v.shape, mybir.dt.from_np(v.dtype), kind="ExternalInput").ap()
           for n, v in arrays.items()]
    out = nc.dram_tensor("out", (B, NQ, D), F32, kind="ExternalOutput").ap()
    program(nc, *ins, out)
    r = run_bass_kernel_spmd(nc, [arrays], core_ids=[0])
    return r.results[0]["out"]
```

```python
from contextlib import ExitStack

import concourse.bass as bass
from concourse import mybir

F32 = mybir.dt.float32
F32R = mybir.dt.float32r
I32 = mybir.dt.int32
U32 = mybir.dt.uint32
ALU = mybir.AluOpType
ACT = mybir.ActivationFunctionType
AX = mybir.AxisListType

P = 128
B = 8
NQ = 256
NK = 1601
D = 256
KC = D // P
H = 16
DH = D // H
PAIRS = H // 2
EPS = 1e-5
QT = NQ // P
KT = -(-NK // P)
VS = DH + 1
VW = H * VS + 32 - VS

CHUNKS = [(0, NQ)] + [(o, 256) for o in range(0, NK - 65, 256)] + [(NK - 66, 66)]
NCH = len(CHUNKS)
RANGES = [(0, 402), (402, 400), (802, 400), (NK - 400, 400)]
NEED = [next(c for c in range(1, NCH) if min(CHUNKS[c][0] + CHUNKS[c][1], NK) >= o + w) for o, w in RANGES]
HQ = H * QT
GROUPS = 4
STEPS = GROUPS * KT


CHUNK_RATE = 1.1
MOST = 4
SCORES_FROM = 6
STACK_STEPS = 3
SCORES_END = 3


def side_order():
    chunk = [("turn", 0), ("turn", 1), ("fc", 0), ("proj", 0), ("resid", 0), ("fc", 1)]
    for c in range(2, NCH):
        chunk += [("fc", c), ("proj", c - 1), ("val", c - 1)]
    chunk += [("proj", NCH - 1), ("val", NCH - 1)]
    score = [("score", n) for n in range(len(RANGES) * HQ)]
    steps = [[] for _ in range(STEPS)]
    done, nc_, ns_ = {}, 0, 0
    for s in range(STEPS - SCORES_END):
        if s % KT == 2:
            steps[s].append(("out", (s // KT - 1) % GROUPS))
        while nc_ < len(chunk) and nc_ <= s * CHUNK_RATE:
            steps[s].append(chunk[nc_])
            done[chunk[nc_]] = s
            nc_ += 1
        quota = min(-(-(len(score) - ns_) // (STEPS - SCORES_END - s)), MOST) if s >= SCORES_FROM else 0
        for _ in range(quota):
            ready = done.get(("proj", NEED[min(ns_, len(score) - 1) // HQ]), STEPS) + STACK_STEPS
            if ns_ < len(score) and s >= ready:
                steps[s].append(score[ns_])
                ns_ += 1
    assert nc_ == len(chunk) and ns_ == len(score), (nc_, ns_)
    steps[STEPS - SCORES_END + 1].append(("turnmax", 0))
    return steps


SIDE = side_order()
UNITS = [u for step in SIDE for u in step]
NU = len(UNITS)
UNIT_AT = {u: n for n, u in enumerate(UNITS)}
CUTS = (0, 0.6)
BANKS = 3
assert NU % BANKS == 0, NU
FIRST_UNIT = [sum(len(x) for x in SIDE[:s]) for s in range(STEPS + 1)]

STACK_DMAS = {c: 6 if c == 0 else 3 for c in range(NCH)}


def runs(u, phase):
    if phase == "end":
        return u == ("out", GROUPS - 1)
    if phase == "first":
        return u != ("out", GROUPS - 1)
    return phase == "beside" or (u[0] == "out") == (phase == "last")


def units_before(n, phase, bank=None):
    return sum(runs(u, phase) for i, u in enumerate(UNITS[:n]) if bank in (None, i % BANKS))


def units_until(b, n, phase, bank=None):
    count = units_before(n, phase, bank)
    if phase != "alone":
        count += units_before(NU, "alone", bank)
    if phase not in ("alone", "first"):
        count += units_before(NU, "first", bank) + (NU if bank is None else NU // BANKS) * ((B if phase == "end" else b) - 2)
    if phase == "end":
        count += units_before(NU, "last", bank)
    return count


def chunk_lead(c):
    return max(CHUNKS[c - 1][0] + CHUNKS[c - 1][1] - CHUNKS[c][0], 0) if c > 1 else 0


def key_tile(kt):
    k0 = kt * P
    c = min(1 + k0 // 256, NCH - 1)
    return c, k0 - CHUNKS[c][0], min(P, NK - k0)


def setup(nc, t, x, weights, w_q, b_v):
    with ExitStack() as tmp:
        wraw = tmp.enter_context(nc.sbuf_tensor("wraw", [P, 3, KC, D], F32))
        xall = tmp.enter_context(nc.sbuf_tensor("xall", [P, B * QT, D], F32))
        stats = tmp.enter_context(nc.sbuf_tensor("stats", [P, B * QT, 6], F32))
        mv = tmp.enter_context(nc.sbuf_tensor("mv", [P, B * QT, 2], F32))
        half = tmp.enter_context(nc.sbuf_tensor("half", [P, B * QT], F32))
        vare = tmp.enter_context(nc.sbuf_tensor("vare", [P, B * QT], F32))
        w_in = [tmp.enter_context(nc.semaphore(f"w_in{i}")) for i in range(3)]
        x_all_in = tmp.enter_context(nc.semaphore("x_all_in"))
        small_in = tmp.enter_context(nc.semaphore("small_in"))
        w_hi_done = tmp.enter_context(nc.semaphore("w_hi_done"))
        w_lo_done = tmp.enter_context(nc.semaphore("w_lo_done"))
        stats_done = tmp.enter_context(nc.semaphore("stats_done"))
        var_done = tmp.enter_context(nc.semaphore("var_done"))
        rstd_done = tmp.enter_context(nc.semaphore("rstd_done"))
        set_done = tmp.enter_context(nc.semaphore("set_done"))
        ones_done = tmp.enter_context(nc.semaphore("ones_done"))
        with nc.Block() as block:

            @block.sync
            def _(sp):
                sp.dma_start(xall[:, :, :], x.rearrange("b (t p) d -> p (b t) d", p=P)).then_inc(x_all_in, 16)
                for i, w in enumerate(weights):
                    sp.dma_start(wraw[:, i, :, :], w.rearrange("(c p) n -> p c n", p=P)).then_inc(w_in[i], 16)
                for i, bias in enumerate(t.bias_in):
                    sp.dma_start(t.bias[:, i, :], bias.rearrange("(c p) -> p c", p=P),
                                 allow_slow_non_contiguous=True).then_inc(small_in, 16)
                sp.dma_start(t.bv[:, :], b_v.partition_broadcast(P)).then_inc(small_in, 16)
                sp.dma_start(t.wq[:, :, :], w_q.rearrange("(c p) n -> p c n", p=P)).then_inc(small_in, 16)
                sp.wait_ge(small_in, 16 * (len(t.bias_in) + 2))

            @block.gpsimd
            def _(pool):
                pool.memset(t.ident[:, :], 0.0).then_inc(set_done, 1)
                pool.memset(half[:, :], -0.5).then_inc(set_done, 1)
                pool.wait_ge(set_done, 1)
                pool.affine_select(out=t.ident[:, :], in_=t.ident[:, :], compare_op=ALU.not_equal, fill=1.0,
                                   base=0, pattern=[[-1, P]], channel_multiplier=1).then_inc(set_done, 1)
                for par in range(2):
                    pool.wait_ge(set_done, 3 + 3 * par)
                    pool.memset(t.qst[par][:, :, :].bitcast(F32), 0.0).then_inc(set_done, 1)
                    pool.wait_ge(set_done, 4 + 3 * par)
                    pool.memset(t.kst[par][96:97, :, :].bitcast(F32), 1.0).then_inc(set_done, 1)
                    pool.wait_ge(set_done, 5 + 3 * par)
                    pool.memset(t.v[par][:, :, :], 1.0).then_inc(set_done, 1)
                pool.wait_ge(var_done, 1)
                pool.wait_ge(set_done, 2)
                pool.tensor_tensor(t.rstd[:, :], vare[:, :], half[:, :], ALU.pow).then_inc(rstd_done, 1)
                pool.wait_ge(rstd_done, 1)
                pool.wait_ge(set_done, 9)

            @block.vector
            def _(dve):
                dve.wait_ge(x_all_in, 16)
                for i in range(B * QT):
                    dve.bn_stats(stats[:, i, :], xall[:, i, :]).then_inc(stats_done, 1)
                dve.wait_ge(stats_done, B * QT)
                for i in range(B * QT):
                    dve.bn_aggr(mv[:, i, :], stats[:, i, :]).then_inc(stats_done, 1)
                dve.wait_ge(stats_done, 2 * B * QT)
                dve.tensor_scalar(vare[:, :], mv[:, :, 1], EPS, None, ALU.add).then_inc(var_done, 1)
                dve.tensor_copy(t.mean[:, :], mv[:, :, 0]).then_inc(var_done, 1)
                for i in range(3):
                    dve.wait_ge(w_hi_done, i + 1)
                    dve.tensor_tensor(t.wlo[:, i, :, :], wraw[:, i, :, :], t.whi[:, i, :, :].bitcast(F32),
                                      ALU.subtract).then_inc(w_lo_done, 1)
                dve.wait_ge(w_lo_done, 3)
                dve.wait_ge(var_done, 2)

            @block.scalar
            def _(act):
                for i in range(3):
                    act.wait_ge(w_in[i], 16)
                    act.activation(t.whi[:, i, :, :], wraw[:, i, :, :], ACT.Copy).then_inc(w_hi_done, 1)


def attention(nc, t, x, ctx_t, x1):
    with ExitStack() as ctx:
        def sb(name, shape, dt):
            return ctx.enter_context(nc.sbuf_tensor(name, shape, dt))

        def sem(name):
            return ctx.enter_context(nc.semaphore(name))

        raw = sb("raw", [P, KC, 256], F32)
        chi = sb("chi", [P, KC, 256], F32R)
        clo = sb("clo", [P, KC, 256], F32R)
        fc = sb("fc", [P, KC, 256], F32)
        fhi = sb("fhi", [P, KC, 256], F32R)
        flo = sb("flo", [P, KC, 256], F32R)
        parts = sb("parts", [P, 2, KC, 256], F32R)
        phi, plo = parts[:, 0, :, :], parts[:, 1, :, :]
        parts_at = nc.dram_tensor("parts_at", [NCH, 2, KC, P, 256], F32).ap()
        xn = fc
        res = [sb(f"res{i}", [P, QT, D], F32) for i in range(2)]
        prob = [sb(f"prob{i}", [P, 4 * NQ], F32) for i in range(2)]
        accsb = sb("accsb", [P, NQ], F32)
        att = accsb[:, 0:P].rearrange("p (q j d) -> p q j d", q=QT, d=DH)
        rec = sb("rec", [P, QT, 4], F32)
        mx = sb("mx", [P, HQ, len(RANGES)], F32)
        mxr = sb("mxr", [P, HQ], F32)
        mrow = sb("mrow", [HQ, P], F32R)
        st = [ctx.enter_context(nc.psum_tensor(f"st{i}", [P, 4 * NQ], F32)) for i in range(2)]
        acc = ctx.enter_context(nc.psum_tensor("acc", [P, 512], F32))
        side = [ctx.enter_context(nc.psum_tensor(f"side{i}", [P, 512], F32)) for i in range(BANKS)]

        side_full = sem("side_full")
        side_free = [sem(f"side_free{i}") for i in range(BANKS)]
        raw_in = sem("raw_in")
        x_in = sem("x_in")
        xn_in = sem("xn_in")
        xn_done = sem("xn_done")
        xb_done = sem("xb_done")
        hi_c = sem("hi_c")
        lo_c = sem("lo_c")
        hi_f = sem("hi_f")
        lo_f = sem("lo_f")
        phi_done = sem("phi_done")
        parts_out = sem("parts_out")
        stack_in = [sem(f"stack_in{c}") for c in range(NCH)]
        row_in = sem("row_in")
        mx_done = sem("mx_done")
        st_full = sem("st_full")
        exp_done = sem("exp_done")
        pv_done = sem("pv_done")
        acc_out = sem("acc_out")
        rec_done = sem("rec_done")
        x1_ready = sem("x1_ready")
        x1_out = sem("x1_out")

        def after(eng, s, value, first):
            if not first:
                eng.wait_ge(s, value)

        def unit_full(eng, b, n, phase):
            eng.wait_ge(side_full, units_until(b, n, phase) + 1)

        def unit_out(eng, b, n, phase):
            eng.wait_ge(side_free[n % BANKS], units_until(b, n, phase, n % BANKS) + 1)

        def out_batch(b, g):
            return b - 1 if g < GROUPS - 1 else b - 2

        def pe_unit(pe, b, par, n, phase):
            kind, c = UNITS[n]
            bank = side[n % BANKS]
            after(pe, side_free[n % BANKS], units_until(b, n, phase, n % BANKS), phase == "alone" and
                  units_before(n, phase, n % BANKS) == 0)
            if kind == "turn":
                pe.wait_ge(xn_done, QT * b + QT)
                for q in range(QT):
                    mm = pe.transpose(bank[:, q * P:(q + 1) * P], xn[:, q, c * P:(c + 1) * P], t.ident[:, :])
            elif kind == "resid":
                for q in range(QT):
                    for k in range(KC):
                        mm = pe.transpose(bank[:, q * D + k * P:q * D + (k + 1) * P],
                                          fc[:, k, q * P:(q + 1) * P], t.ident[:, :])
            elif kind == "proj" and c == 0:
                unit_out(pe, b, UNIT_AT["fc", 0], phase)
                for m in range(KC):
                    for k in range(KC):
                        mm = pe.matmul(bank[:, m * 256:m * 256 + NQ], t.wq[:, k, m * P:(m + 1) * P], fc[:, k, :],
                                       start=(k == 0), stop=(k == KC - 1))
            elif kind in ("fc", "proj"):
                w = CHUNKS[c][1]
                if kind == "fc":
                    pe.wait_ge(lo_c, NCH * b + c + 1)
                    wi, hi, lo = 0, chi, clo
                else:
                    pe.wait_ge(lo_f, (NCH - 1) * b + c)
                    wi, hi, lo = 1, fhi, flo
                for m in range(KC):
                    i = 0
                    for k in range(KC):
                        for wt, mov in ((t.whi, hi), (t.whi, lo), (t.wlo, hi)):
                            mm = pe.matmul(bank[:, m * 256:m * 256 + w], wt[:, wi, k, m * P:(m + 1) * P],
                                           mov[:, k, 0:w], start=(i == 0), stop=(i == 3 * KC - 1))
                            i += 1
            elif kind == "val":
                pe.wait_ge(lo_f, (NCH - 1) * b + c)
                tiles = [kt for kt in range(KT) if key_tile(kt)[0] == c]
                for j, kt in enumerate(tiles):
                    _, o, rows = key_tile(kt)
                    i = 0
                    for k in range(KC):
                        for a, wt in ((fhi, t.whi), (fhi, t.wlo), (flo, t.whi)):
                            mm = pe.matmul(bank[0:rows, j * D:(j + 1) * D], a[:, k, o:o + rows],
                                           wt[:, 2, k, :], start=(i == 0), stop=(i == 3 * KC - 1))
                            i += 1
            elif kind == "score":
                r, hq = divmod(c, HQ)
                if hq == 0:
                    o, w = RANGES[r]
                    for i in range(NEED[r - 1] + 1 if r else 0, NEED[r] + 1):
                        pe.wait_ge(stack_in[i], 16 * STACK_DMAS[i] * (b + 1))
                o, w = RANGES[r]
                mm = pe.matmul(bank[:, 0:w], t.qst[par][0:96, hq // 4, (hq % 4) * P:(hq % 4 + 1) * P],
                               t.kst[par][0:96, hq // 4, o:o + w], start=True, stop=True)
            elif kind == "out":
                pe.wait_ge(acc_out, GROUPS * out_batch(b, c) + c + 1)
                for q in range(QT):
                    mm = pe.transpose(bank[:, q * P:(q + 1) * P], accsb[:, q * P:(q + 1) * P], t.ident[:, :])
            else:
                pe.wait_ge(mx_done, b + 1)
                mm = pe.transpose(bank[0:HQ, 0:P], mxr[:, :], t.ident[:, :])
            mm.then_inc(side_full, 1)

        def act_load(act, b, c):
            o, w = CHUNKS[c]
            act.wait_ge(lo_c, NCH * b + c)
            act.dma_start(raw[:, :, 0:w], ctx_t[b].rearrange("(k p) n -> p k n", p=P)[:, :, o:o + w])\
               .then_inc(raw_in, 16)

        def act_chunk_high(act, c):
            w = CHUNKS[c][1]
            act.activation(chi[:, :, 0:w], raw[:, :, 0:w], ACT.Copy).then_inc(hi_c, 1)

        def act_fc_high(act, b, c, phase):
            w = CHUNKS[c][1]
            unit_out(act, b, UNIT_AT["fc", c], phase)
            act.activation(fhi[:, :, 0:w], fc[:, :, 0:w], ACT.Copy).then_inc(hi_f, 1)

        def act_unit(act, b, par, n, phase):
            kind, c = UNITS[n]
            bank, free = side[n % BANKS], side_free[n % BANKS]
            first = phase == "alone"
            if kind in ("resid", "score", "out"):
                return
            unit_full(act, b, n, phase)
            if kind == "turn":
                after(act, lo_c, NCH * b, first)
                act.activation(raw[:, c, :], bank[:, 0:NQ], ACT.Copy).then_inc(free, 1)
                if c == KC - 1:
                    for k in range(KC):
                        unit_out(act, b, UNIT_AT["turn", k], phase)
                    act_chunk_high(act, 0)
                    act_load(act, b, 1)
            elif kind == "fc":
                w = CHUNKS[c][1]
                if c == 1:
                    unit_full(act, b, UNIT_AT["resid", 0], phase)
                else:
                    after(act, lo_f, (NCH - 1) * b + max(c - 1, 0), first and c == 0)
                for m in range(KC):
                    op = act.activation(fc[:, m, 0:w], bank[:, m * 256:m * 256 + w], ACT.Relu,
                                        bias=t.bias[:, 0, m:m + 1])
                op.then_inc(free, 1)
                if c + 1 < NCH:
                    act.wait_ge(raw_in, 16 * ((NCH - 1) * b + c + 1))
                    act_chunk_high(act, c + 1)
                if c == 1:
                    act_fc_high(act, b, 1, phase)
                if c < 2:
                    act_load(act, b, c + 2)
            elif kind == "proj":
                w = CHUNKS[c][1]
                after(act, parts_out, 16 * (NCH * b + c), first and c == 0)
                for m in range(KC):
                    op = act.activation(phi[:, m, 0:w], bank[:, m * 256:m * 256 + w], ACT.Identity,
                                        bias=t.bias[:, 1 if c == 0 else 2, m:m + 1])
                op.then_inc(phi_done, 1)
                if 0 < c < NCH - 3:
                    act_load(act, b, c + 3)
            elif kind == "val":
                tiles = [kt for kt in range(KT) if key_tile(kt)[0] == c]
                rows = key_tile(tiles[0])[2]
                k = len(tiles)
                dst = t.v[par][0:rows, tiles[0]:tiles[0] + k, 0:H * VS].rearrange("p k (h s) -> p k h s", s=VS)
                act.activation(dst[:, :, :, 0:DH],
                               bank[0:rows, 0:k * D].rearrange("p (k h s) -> p k h s", k=k, s=DH),
                               ACT.Copy).then_inc(free, 1)
                if c + 1 < NCH:
                    act_fc_high(act, b, c + 1, phase)
            else:
                after(act, row_in, 16 * b, first)
                act.activation(mrow[:, :], bank[0:HQ, 0:P], ACT.Copy, scale=-1.0).then_inc(free, 1)

        def dve_unit(dve, b, par, n, phase):
            kind, c = UNITS[n]
            bank, free = side[n % BANKS], side_free[n % BANKS]
            if kind == "resid":
                unit_full(dve, b, n, phase)
                dve.wait_ge(xb_done, b + 1)
                dve.tensor_tensor(res[par][:, :, :], bank[:, :].rearrange("p (q d) -> p q d", q=QT),
                                  res[par][:, :, :], ALU.add).then_inc(free, 1)
            elif kind == "proj":
                w = CHUNKS[c][1]
                dve.wait_ge(phi_done, NCH * b + c + 1)
                for m in range(KC):
                    op = dve.scalar_tensor_tensor(plo[:, m, 0:w], in0=bank[:, m * 256:m * 256 + w],
                                                  scalar=t.bias[:, 1 if c == 0 else 2, m:m + 1],
                                                  in1=phi[:, m, 0:w].bitcast(F32), op0=ALU.add, op1=ALU.subtract)
                op.then_inc(free, 1)
            elif kind == "score":
                r, hq = divmod(c, HQ)
                unit_full(dve, b, n, phase)
                dve.tensor_reduce(mx[:, hq, r:r + 1], bank[:, 0:RANGES[r][1]], AX.X, ALU.max)\
                   .then_inc(free, 1)
                if c == len(RANGES) * HQ - 1:
                    unit_out(dve, b, n, phase)
                    for k in range(1, BANKS):
                        unit_out(dve, b, n - k, phase)
                    dve.tensor_reduce(mxr[:, :], mx[:, :, :], AX.X, ALU.max).then_inc(mx_done, 1)
            elif kind == "out":
                dve_normalise(dve, out_batch(b, c), 1 - par if c < GROUPS - 1 else par, b, n, phase)

        def dve_normalise_input(dve, b, par):
            dve.wait_ge(xn_in, 16 * (b + 1))
            for q in range(QT):
                mean, rstd = t.mean[:, bass.ds(QT * b + q, 1)], t.rstd[:, bass.ds(QT * b + q, 1)]
                dve.tensor_scalar(xn[:, q, :], xn[:, q, :], mean, rstd, ALU.subtract, ALU.mult).then_inc(xn_done, 1)

        def pool_side(pool, b, par, first):
            def low_chunk(c):
                w = CHUNKS[c][1]
                pool.wait_ge(hi_c, NCH * b + c + 1)
                pool.tensor_tensor(clo[:, :, 0:w], raw[:, :, 0:w], chi[:, :, 0:w].bitcast(F32),
                                   ALU.subtract).then_inc(lo_c, 1)

            def low_fc(c):
                w = CHUNKS[c][1]
                pool.wait_ge(hi_f, (NCH - 1) * b + c)
                pool.tensor_tensor(flo[:, :, 0:w], fc[:, :, 0:w], fhi[:, :, 0:w].bitcast(F32),
                                   ALU.subtract).then_inc(lo_f, 1)

            after(pool, lo_f, (NCH - 1) * b, first)
            pool.dma_start(xn[:, :, :], x[b].rearrange("(t p) d -> p t d", p=P)).then_inc(xn_in, 16)
            low_chunk(0)
            for c in range(NCH):
                if c + 1 < NCH:
                    low_chunk(c + 1)
                if c == 0:
                    pool.wait_ge(x_in, 16 * (b + 1))
                    for q in range(QT):
                        op = pool.tensor_tensor(res[par][:, q, :], res[par][:, q, :], t.bv[:, :], ALU.add)
                    op.then_inc(xb_done, 1)
                if c > 0:
                    low_fc(c)

        def sp_load_x(sp, b, par, first):
            after(sp, x1_out, 16 * (b - 1), first)
            sp.dma_start(res[par][:, :, :], x[b].rearrange("(t p) d -> p t d", p=P)).then_inc(x_in, 16)

        def sp_side(sp, b, par, phase):
            for c in range(NCH):
                sp_stack(sp, b, par, c, phase)
            unit_out(sp, b, UNIT_AT["turnmax", 0], phase)
            sp.dma_start(t.qst[par][96:97, :, :].rearrange("p a n -> p (a n)").bitcast(F32),
                         mrow[:, :].bitcast(F32)).then_inc(row_in, 16)

        def sp_stack(sp, b, par, c, phase):
            w = CHUNKS[c][1]
            at = parts_at[c]
            unit_out(sp, b, UNIT_AT["proj", c], phase)
            sp.dma_start(at[:, :, :, 0:w].rearrange("a k q n -> q (a k) n"),
                         parts[:, :, :, 0:w].rearrange("q a k n -> q (a k) n").bitcast(F32)).then_inc(parts_out, 16)
            sp.wait_ge(parts_out, 16 * (NCH * b + c + 1))
            rows = at.rearrange("a k (p r) n -> a r (k p) n", r=32)
            for g, part in enumerate((0, 0, 1) if c == 0 else (0, 1, 0)):
                if c == 0:
                    for j in range(2):
                        sp.dma_start(t.qst[par][32 * g + 16 * j:32 * g + 16 * j + 16, :, j * NQ:(j + 1) * NQ]
                                     .bitcast(F32), rows[part, 16 * j:16 * j + 16, :, 0:NQ]).then_inc(stack_in[c], 16)
                else:
                    o, lead = CHUNKS[c][0], chunk_lead(c)
                    sp.dma_start(t.kst[par][32 * g:32 * g + 32, :, o + lead:o + w].bitcast(F32),
                                 rows[part, :, :, lead:w]).then_inc(stack_in[c], 16)

        def pe_scores(pe, b, par, s, first, between):
            g, kt = divmod(s, KT)
            rows = key_tile(kt)[2]
            if s == 0:
                pe.wait_ge(row_in, 16 * (b + 1))
            after(pe, exp_done, STEPS * b + s - 1, first and s < 2)
            for i in range(2):
                if i:
                    between()
                mm = pe.matmul(st[s % 2][0:rows, i * 2 * NQ:(i + 1) * 2 * NQ],
                               t.kst[par][0:97, 2 * g + i, kt * P:kt * P + rows],
                               t.qst[par][0:97, 2 * g + i, :], start=True, stop=True)
            mm.then_inc(st_full, 1)

        def pe_values(pe, b, par, s, first):
            g, kt = divmod(s, KT)
            rows = key_tile(kt)[2]
            pe.wait_ge(exp_done, STEPS * b + s + 1)
            if kt == 0:
                after(pe, acc_out, GROUPS * b + g, first and g == 0)
            for j in range(4):
                h = 4 * g + j
                mm = pe.matmul(acc[32 * j:32 * j + 32, 0:NQ], t.v[par][0:rows, kt, VS * h:VS * h + 32],
                               prob[s % 2][0:rows, j * NQ:(j + 1) * NQ], start=(kt == 0), stop=(kt == KT - 1))
            mm.then_inc(pv_done, 1)

        def dve_acc_out(dve, b, g, first):
            dve.wait_ge(pv_done, STEPS * b + KT * (g + 1))
            after(dve, x1_ready, GROUPS * b + g, first and g == 0)
            dve.tensor_copy(accsb[:, :], acc[:, 0:NQ]).then_inc(acc_out, 1)

        def dve_normalise(dve, a, par, b, n, phase):
            g = UNITS[n][1]
            unit_full(dve, b, n, phase)
            o = side[n % BANKS][:, 0:NQ].rearrange("p (q j s) -> p q j s", q=QT, s=32)
            dve.reciprocal(rec[:, :, :], o[:, :, :, DH]).then_inc(rec_done, 1)
            dve.wait_ge(rec_done, GROUPS * a + g + 1)
            dve.tensor_tensor(att, o[:, :, :, 0:DH], rec[:, :, :].unsqueeze(3).broadcast_to([P, QT, 4, DH]),
                              ALU.mult).then_inc(side_free[n % BANKS], 1)
            unit_out(dve, b, n, phase)
            r = res[par][:, :, g * 4 * DH:(g + 1) * 4 * DH]
            dve.tensor_tensor(r, r, att.rearrange("p q j s -> p q (j s)"), ALU.add)\
               .then_inc(x1_ready, 1)

        def sp_store(sp, b, par):
            sp.wait_ge(x1_ready, GROUPS * (b + 1))
            sp.dma_start(x1[b].rearrange("(t p) d -> p t d", p=P), res[par][:, :, :]).then_inc(x1_out, 16)

        def batches(eng, body):
            body(0, 0, True, False)
            with eng.Fori(0, B // 2 - 1) as i:
                body(2 * i + 1, 1, False, False)
                body(2 * i + 2, 0, False, False)
            body(B - 1, 1, False, True)

        def phase_of(first, last):
            return "first" if first else "last" if last else "beside"

        def units_of(s, phase):
            return [n for n in range(FIRST_UNIT[s], FIRST_UNIT[s + 1]) if runs(UNITS[n], phase)]

        ALONE = [n for n in range(NU) if UNITS[n][0] != "out"]

        with nc.Block() as block:

            @block.sync
            def _(sp):
                def body(b, par, first, last):
                    if not first:
                        sp_store(sp, b - 1, 1 - par)
                    if not last:
                        sp_load_x(sp, b + 1, 1 - par, first)
                        sp_side(sp, b + 1, 1 - par, phase_of(first, last))

                sp_load_x(sp, 0, 0, True)
                sp_side(sp, 0, 0, "alone")
                batches(sp, body)
                sp_store(sp, B - 1, 1)
                sp.wait_ge(x1_out, 16 * B)

            @block.gpsimd
            def _(pool):
                pool_side(pool, 0, 0, True)
                with pool.Fori(0, B // 2 - 1) as i:
                    pool_side(pool, 2 * i + 1, 1, False)
                    pool_side(pool, 2 * i + 2, 0, False)
                pool_side(pool, B - 1, 1, False)

            @block.scalar
            def _(act):
                def body(b, par, first, last):
                    for s in range(STEPS):
                        rows = key_tile(s % KT)[2]
                        act.wait_ge(st_full, STEPS * b + s + 1)
                        after(act, pv_done, STEPS * b + s - 1, first and s < 2)
                        act.activation(prob[s % 2][0:rows, :], st[s % 2][0:rows, :], ACT.Exp,
                                       scale=float(DH) ** -0.5).then_inc(exp_done, 1)
                        for n in units_of(s, phase_of(first, last)):
                            act_unit(act, b + 1, 1 - par, n, phase_of(first, last))

                for n in ALONE:
                    act_unit(act, 0, 0, n, "alone")
                batches(act, body)

            @block.vector
            def _(dve):
                def body(b, par, first, last):
                    if not last:
                        dve_normalise_input(dve, b + 1, 1 - par)
                    for s in range(STEPS):
                        g, kt = divmod(s, KT)
                        if kt == 1 and g > 0:
                            dve_acc_out(dve, b, g - 1, first)
                        for n in units_of(s, phase_of(first, last)):
                            dve_unit(dve, b + 1, 1 - par, n, phase_of(first, last))
                    dve_acc_out(dve, b, GROUPS - 1, first)

                dve_normalise_input(dve, 0, 0)
                for n in ALONE:
                    dve_unit(dve, 0, 0, n, "alone")
                batches(dve, body)
                dve_unit(dve, B + 1, 1, UNIT_AT["out", GROUPS - 1], "end")

            @block.tensor
            def _(pe):
                def body(b, par, first, last):
                    phase = phase_of(first, last)
                    for s in range(STEPS):
                        units = units_of(s, phase)
                        k = len(units)
                        cut = [round(k * f) for f in CUTS]

                        def side_units(part):
                            for n in units[part]:
                                pe_unit(pe, b + 1, 1 - par, n, phase)

                        pe_scores(pe, b, par, s, first, lambda: side_units(slice(0, cut[0])))
                        side_units(slice(cut[0], cut[1]))
                        if s > 0:
                            pe_values(pe, b, par, s - 1, first)
                        side_units(slice(cut[1], k))
                    pe_values(pe, b, par, STEPS - 1, first)

                for n in ALONE:
                    pe_unit(pe, 0, 0, n, "alone")
                batches(pe, body)
                pe_unit(pe, B + 1, 1, UNIT_AT["out", GROUPS - 1], "end")


I = 512
E = 8
TOP = 2
FT = I // P
N = B * NQ
T = N // P
TW = 512
TC = N // TW
SLOT_TILES = -(-(TOP * N // P + E - 1) // 4) * 4
RING = 4
ROUNDS = SLOT_TILES // RING
ROW = D + 2
WE = KC * 2 * I + FT * D
WD = KC * 2 * I


def ffn(nc, ident, x1, gate_w, gate_up, down, out):
    slot_x = nc.dram_tensor("slot_x", [SLOT_TILES * P, ROW], F32).ap()
    part = nc.dram_tensor("part", [TOP * N + SLOT_TILES * P, D], F32).ap()
    with ExitStack() as ctx:
        def sb(name, shape, dt=F32):
            return ctx.enter_context(nc.sbuf_tensor(name, shape, dt))

        def sem(name):
            return ctx.enter_context(nc.semaphore(name))

        def bank(name):
            return ctx.enter_context(nc.psum_tensor(name, [P, 512], F32))

        y = sb("y", [P, T, D])
        rows = sb("rows", [P, T, ROW])
        xnt = sb("xnt", [P, KC, N])
        wall = sb("wall", [P, E * WE])
        wb = sb("wb", [P, WE])
        h = sb("h", [P, FT, TW])
        sil = [sb(f"sil{i}", [P, TW]) for i in range(2)]
        zeros = sb("zeros", [P, D])
        unused = sb("unused", [P, SLOT_TILES, 2])
        gw = sb("gw", [P, KC, E])
        lt = h[0:E, :, :].rearrange("p a b -> p (a b)")
        stats = sb("stats2", [P, T, 6])
        mv = sb("mv2", [P, T, 2])
        vare = sb("vare2", [P, T])
        held = sb("held", [1, SLOT_TILES])
        half = sb("half2", [P, T])
        rstd = sb("rstd2", [P, T])
        top = sb("top", [P, T])
        ex = sb("ex", [P, T, E])
        pr = sb("pr", [P, T, E])
        beats = sb("beats", [P, T, E, E])
        rank = sb("rank", [P, T, E])
        sel = sb("sel", [P, T, E])
        comb = sb("comb", [P, T, E])
        below = sb("below", [P, P])
        ones = sb("ones", [P, P])
        scan = [sb(f"scan{i}", [P, T, E]) for i in range(2)]
        count = sb("count", [P, E])
        iota16 = sb("iota16", [P, T])
        tiles = [sb(f"tiles{i}", [P, E]) for i in range(2)]
        iota40 = sb("iota40", [1, SLOT_TILES])
        ends = sb("ends", [1, SLOT_TILES, E])
        expert_f = sb("expert_f", [1, SLOT_TILES])
        expert = sb("expert", [1, SLOT_TILES], I32)
        slot = sb("slot", [P, T, E])
        pick = sb("pick", [P, T, E])
        slot_f = sb("slot_f", [P, T, TOP])
        slots = sb("slots", [P, T, TOP], U32)
        weight = sb("weight", [P, T, TOP])
        goal = sb("goal", [P, T, TOP], U32)
        xg = [sb(f"xg{i}", [P, ROW]) for i in range(RING)]
        xgt = [sb(f"xgt{i}", [P, KC, P]) for i in range(2)]
        sg = sb("sg", [P, I])
        hg = sb("hg", [P, I])
        hgt = sb("hgt", [P, FT, P])
        yg = [sb(f"yg{i}", [P, D]) for i in range(RING)]
        first_part = wall[:, 0:T * D].rearrange("p (t d) -> p t d", d=D)
        second_part = wall[:, T * D:2 * T * D].rearrange("p (t d) -> p t d", d=D)
        pg = [bank(f"pg{i}") for i in range(2)]
        pu = [bank(f"pu{i}") for i in range(2)]
        py = [bank(f"py{i}") for i in range(4)]

        y_in = sem("y_in")
        gw_in = sem("gw_in")
        wb_in = sem("wb_in")
        wall_in = sem("wall_in")
        empty_out = sem("empty_out")
        consts = sem("consts")
        out_done = sem("out_done")
        st_done = sem("st_done")
        v_done = sem("v_done")
        r_done = sem("r_done")
        n_done = sem("n_done")
        turned = sem("turned")
        xnt_done = sem("xnt_done")
        logit_full = sem("logit_full")
        lt_done = sem("lt_done")
        lt_turned = sem("lt_turned")
        chain = sem("chain")
        sub_done = sem("sub_done")
        gate_exp = sem("gate_exp")
        sel_done = sem("sel_done")
        count_full = sem("count_full")
        expert_done = sem("expert_done")
        rows_ready = sem("rows_ready")
        rows_out = sem("rows_out")
        g_full = sem("g_full")
        sil_done = sem("sil_done")
        h_done = sem("h_done")
        y_full = sem("y_full")
        y_done = sem("y_done")
        xg_in = [sem(f"xg_in{i}") for i in range(RING)]
        xg_turned = sem("xg_turned")
        xgt_done = sem("xgt_done")
        gate_full = sem("gate_full")
        up_full = sem("up_full")
        sg_done = sem("sg_done")
        hg_done = sem("hg_done")
        hg_turned = sem("hg_turned")
        hgt_done = sem("hgt_done")
        yg_full = sem("yg_full")
        yg_done = sem("yg_done")
        yg_out = [sem(f"yg_out{i}") for i in range(RING)]
        part_in = sem("part_in")
        sum_done = sem("sum_done")

        def after(eng, s, value, first):
            if not first:
                eng.wait_ge(s, value)

        def before(i, r):
            return (i, r - 1) if r else (i - 1, RING - 1)

        def behind(i, r):
            return (i, r + 1) if r + 1 < RING else (i + 1, 0)

        def slot_tiles(eng, body):
            for r in range(RING):
                body(0, r, True)
            with eng.Fori(1, ROUNDS) as i:
                for r in range(RING):
                    body(i, r, False)

        with nc.Block() as block:

            @block.sync
            def _(sp):
                sp.dma_start(y[:, :, :], x1.rearrange("b (t p) d -> p (b t) d", p=P)).then_inc(y_in, 16)
                sp.dma_start(gw[:, :, :], gate_w.rearrange("(k p) e -> p k e", p=P)).then_inc(gw_in, 16)
                sp.wait_ge(consts, 6)
                sp.dma_start(slot_x.rearrange("(t p) r -> p t r", p=P)[:, :, 0:D],
                             zeros[:, :].unsqueeze(1).broadcast_to([P, SLOT_TILES, D])).then_inc(empty_out, 16)
                sp.dma_start(slot_x.rearrange("(t p) r -> p t r", p=P)[:, :, D:ROW], unused[:, :, :])\
                  .then_inc(empty_out, 16)

                def load(w, e, s):
                    sp.dma_start(w[:, 0:WD].rearrange("p (k n) -> p k n", k=KC),
                                 gate_up[e].rearrange("(k p) n -> p k n", p=P)).then_inc(s, 16)
                    sp.dma_start(w[:, WD:WE].rearrange("p (k n) -> p k n", k=FT),
                                 down[e].rearrange("(k p) n -> p k n", p=P)).then_inc(s, 16)

                load(wb, E, wb_in)
                for e in range(E):
                    load(wall[:, e * WE:(e + 1) * WE], e, wall_in)
                sp.wait_ge(rows_out, 16 * TOP * T)

                def body(i, r, first):
                    after(sp, yg_out[r], 16 * i, first)
                    sp.dma_start(xg[r][:, :], slot_x[bass.ds((RING * i + r) * P, P), :]).then_inc(xg_in[r], 16)

                slot_tiles(sp, body)
                for r in range(RING):
                    sp.wait_ge(yg_out[r], 16 * ROUNDS)
                for a, o in ((first_part, 0), (second_part, N)):
                    sp.dma_start(a, part[o:o + N, :].rearrange("(t p) d -> p t d", p=P)).then_inc(part_in, 16)
                for k in range(4):
                    sp.wait_ge(sum_done, k + 1)
                    sp.dma_start(out.rearrange("b (t p) d -> p (b t) d", p=P)[:, 4 * k:4 * k + 4, :],
                                 y[:, 4 * k:4 * k + 4, :]).then_inc(out_done, 16)
                sp.wait_ge(out_done, 64)

            @block.gpsimd
            def _(pool):
                pool.memset(half[:, :], -0.5).then_inc(consts, 1)
                pool.memset(ones[:, :], 1.0).then_inc(consts, 1)
                pool.memset(zeros[:, :], 0.0).then_inc(consts, 1)
                pool.memset(unused[:, :, :], 0.0).then_inc(consts, 1)
                pool.wait_ge(consts, 4)
                pool.affine_select(out=below[:, :], in_=ones[:, :], compare_op=ALU.is_gt, fill=0.0,
                                   base=0, pattern=[[1, P]], channel_multiplier=-1).then_inc(consts, 1)
                pool.iota(unused[:, :, 1:2].bitcast(U32), [[P, SLOT_TILES], [1, 1]], base=TOP * N,
                          channel_multiplier=1).then_inc(consts, 1)
                pool.iota(iota16[:, :], [[P, T]], base=0, channel_multiplier=0,
                          allow_small_or_imprecise_dtypes=True).then_inc(consts, 1)
                pool.iota(iota40[:, :], [[1, SLOT_TILES]], base=0, channel_multiplier=0,
                          allow_small_or_imprecise_dtypes=True).then_inc(consts, 1)
                pool.iota(goal[:, :, :], [[P, T], [N, TOP]], base=0, channel_multiplier=1).then_inc(consts, 1)
                pool.wait_ge(v_done, 1)
                pool.tensor_tensor(rstd[:, :], vare[:, :], half[:, :], ALU.pow).then_inc(r_done, 1)
                pool.wait_ge(empty_out, 32)
                for k in range(TOP):
                    pool.wait_ge(rows_ready, k + 1)
                    for t in range(T):
                        pool.indirect_dma_start(
                            out=slot_x, out_offset=bass.IndirectOffsetOnAxis(ap=slots[:, t, k:k + 1], axis=0),
                            in_=rows[:, t, :], in_offset=None).then_inc(rows_out, 16)

                def body(i, r, first):
                    pool.wait_ge(yg_done, RING * i + r + 1)
                    pool.tensor_tensor(held[:, bass.ds(RING * i + r, 1)], half[0:1, 0:1], half[0:1, 0:1], ALU.add)
                    pool.indirect_dma_start(
                        out=part, out_offset=bass.IndirectOffsetOnAxis(ap=xg[r][:, D + 1:D + 2].bitcast(U32), axis=0),
                        in_=yg[r][:, :], in_offset=None).then_inc(yg_out[r], 16)

                slot_tiles(pool, body)

            @block.vector
            def _(dve):
                links = [0]

                def link(op):
                    links[0] += 1
                    op.then_inc(chain, 1)
                    dve.wait_ge(chain, links[0])

                dve.wait_ge(y_in, 16)
                for i in range(T):
                    dve.bn_stats(stats[:, i, :], y[:, i, :]).then_inc(st_done, 1)
                dve.wait_ge(st_done, T)
                for i in range(T):
                    dve.bn_aggr(mv[:, i, :], stats[:, i, :]).then_inc(st_done, 1)
                dve.wait_ge(st_done, 2 * T)
                dve.tensor_scalar(vare[:, :], mv[:, :, 1], EPS, None, ALU.add).then_inc(v_done, 1)
                dve.wait_ge(r_done, 1)
                for i in range(T):
                    dve.tensor_scalar(rows[:, i, 0:D], y[:, i, :], mv[:, i, 0:1], rstd[:, i:i + 1],
                                      ALU.subtract, ALU.mult).then_inc(n_done, 1)
                dve.wait_ge(lt_turned, 1)
                logits = pg[0][:, 0:T * E].rearrange("p (t e) -> p t e", e=E)

                def by_token(a):
                    return a[:, :].unsqueeze(2).broadcast_to([P, T, E])

                link(dve.tensor_reduce(top[:, :], logits, AX.X, ALU.max))
                dve.tensor_tensor(ex[:, :, :], logits, by_token(top), ALU.subtract).then_inc(sub_done, 1)
                dve.wait_ge(gate_exp, 1)
                link(dve.tensor_reduce(top[:, :], ex[:, :, :], AX.X, ALU.add))
                link(dve.reciprocal(top[:, :], top[:, :]))
                link(dve.tensor_tensor(pr[:, :, :], ex[:, :, :], by_token(top), ALU.mult))
                for e in range(E):
                    if e > 0:
                        dve.tensor_tensor(beats[:, :, e, 0:e], pr[:, :, e:e + 1].broadcast_to([P, T, e]),
                                          pr[:, :, 0:e], ALU.is_gt)
                    op = dve.tensor_tensor(beats[:, :, e, e:E], pr[:, :, e:e + 1].broadcast_to([P, T, E - e]),
                                           pr[:, :, e:E], ALU.is_ge)
                link(op)
                link(dve.tensor_reduce(rank[:, :, :], beats[:, :, :, :].rearrange("p t a b -> p t b a"), AX.X,
                                       ALU.add))
                dve.tensor_scalar(sel[:, :, :], rank[:, :, :], TOP + 0.5, None, ALU.is_lt).then_inc(sel_done, 1)
                dve.wait_ge(sel_done, 1)
                link(dve.tensor_tensor(comb[:, :, :], sel[:, :, :], pr[:, :, :], ALU.mult))
                link(dve.tensor_reduce(top[:, :], comb[:, :, :], AX.X, ALU.add))
                link(dve.reciprocal(top[:, :], top[:, :]))
                link(dve.tensor_tensor(comb[:, :, :], comb[:, :, :], by_token(top), ALU.mult))
                dve.wait_ge(count_full, 1)
                total = pg[1][:, T * E:2 * T * E].rearrange("p (t e) -> p t e", e=E)
                within = pg[1][:, 0:T * E].rearrange("p (t e) -> p t e", e=E)
                link(dve.tensor_copy(scan[0][:, :, :], total))
                a, step = 0, 1
                while step < T:
                    dve.tensor_copy(scan[1 - a][:, 0:step, :], scan[a][:, 0:step, :])
                    link(dve.tensor_tensor(scan[1 - a][:, step:T, :], scan[a][:, step:T, :],
                                           scan[a][:, 0:T - step, :], ALU.add))
                    a, step = 1 - a, 2 * step
                upto = scan[a]
                link(dve.tensor_copy(count[:, :], upto[:, T - 1, :]))
                link(dve.tensor_tensor(pick[:, :, :], count[:, :].unsqueeze(1).broadcast_to([P, T, E]),
                                       iota16[:, :].unsqueeze(2).broadcast_to([P, T, E]), ALU.is_gt))
                link(dve.tensor_reduce(tiles[0][:, :], pick[:, :, :].rearrange("p t e -> p e t"), AX.X, ALU.add))
                b, step = 0, 1
                while step < E:
                    dve.tensor_copy(tiles[1 - b][:, 0:step], tiles[b][:, 0:step])
                    link(dve.tensor_tensor(tiles[1 - b][:, step:E], tiles[b][:, step:E], tiles[b][:, 0:E - step],
                                           ALU.add))
                    b, step = 1 - b, 2 * step
                ended = tiles[b]
                link(dve.tensor_tensor(ends[:, :, :], iota40[:, :].unsqueeze(2).broadcast_to([1, SLOT_TILES, E]),
                                       ended[0:1, :].unsqueeze(1).broadcast_to([1, SLOT_TILES, E]), ALU.is_ge))
                link(dve.tensor_reduce(expert_f[:, :], ends[:, :, :], AX.X, ALU.add))
                dve.tensor_scalar(expert[:, :], expert_f[:, :], float(E - 1), None, ALU.min).then_inc(expert_done, 1)
                link(dve.tensor_tensor(slot[:, :, :], within, upto[:, :, :], ALU.add))
                link(dve.tensor_tensor(slot[:, :, :], slot[:, :, :], total, ALU.subtract))
                link(dve.scalar_tensor_tensor(slot[:, :, 1:E], in0=ended[:, 0:E - 1].unsqueeze(1)
                                              .broadcast_to([P, T, E - 1]), scalar=float(P),
                                              in1=slot[:, :, 1:E], op0=ALU.mult, op1=ALU.add))
                for k in range(TOP):
                    for src, dst in ((slot, slot_f), (comb, weight)):
                        link(dve.scalar_tensor_tensor(pick[:, :, :], in0=rank[:, :, :], scalar=float(k + 1),
                                                      in1=src[:, :, :], op0=ALU.is_equal, op1=ALU.mult))
                        link(dve.tensor_reduce(dst[:, :, k], pick[:, :, :], AX.X, ALU.add))
                link(dve.tensor_copy(slots[:, :, :], slot_f[:, :, :]))
                for k in range(TOP):
                    after(dve, rows_out, 16 * T * k, k == 0)
                    link(dve.tensor_copy(rows[:, :, D:D + 1], weight[:, :, k:k + 1]))
                    dve.tensor_copy(rows[:, :, D + 1:D + 2].bitcast(U32), goal[:, :, k:k + 1])\
                       .then_inc(rows_ready, 1)

                for c in range(TC):
                    for f in range(FT):
                        dve.wait_ge(sil_done, FT * c + f + 1)
                        if f == 0 and c > 0:
                            dve.wait_ge(y_full, 4 * c)
                        dve.tensor_tensor(h[:, f, :], sil[f % 2][:, :], pu[f % 2][:, :], ALU.mult).then_inc(h_done, 1)
                    for q in range(4):
                        t = 4 * c + q
                        dve.wait_ge(y_full, 4 * c + q + 1)
                        dve.tensor_tensor(y[:, t, :], py[q][:, 0:D], y[:, t, :], ALU.add).then_inc(y_done, 1)

                def scaled(i, r, first):
                    dve.wait_ge(yg_full, RING * i + r + 1)
                    after(dve, yg_out[r], 16 * i, first)
                    dve.tensor_scalar(yg[r][:, :], py[1][:, 0:D], xg[r][:, D:D + 1], None, ALU.mult)\
                       .then_inc(yg_done, 1)

                def body(i, r, first):
                    n = RING * i + r
                    begin = first and r == 0
                    dve.wait_ge(sg_done, n + 1)
                    dve.wait_ge(up_full, n + 1)
                    after(dve, hg_turned, n, begin)
                    dve.tensor_tensor(hg[:, :], sg[:, :], pu[0][:, :], ALU.mult).then_inc(hg_done, 1)
                    if not begin:
                        scaled(*before(i, r), first)

                slot_tiles(dve, body)
                scaled(ROUNDS - 1, RING - 1, False)
                dve.wait_ge(part_in, 32)
                for k in range(4):
                    q = slice(4 * k, 4 * k + 4)
                    link(dve.tensor_tensor(y[:, q, :], y[:, q, :], first_part[:, q, :], ALU.add))
                    dve.tensor_tensor(y[:, q, :], y[:, q, :], second_part[:, q, :], ALU.add).then_inc(sum_done, 1)

            @block.scalar
            def _(act):
                for i in range(T):
                    act.wait_ge(turned, i + 1)
                    act.activation(xnt[:, :, i * P:(i + 1) * P],
                                   py[i % 4][:, 0:D].rearrange("p (k q) -> p k q", k=KC), ACT.Copy)\
                       .then_inc(xnt_done, 1)
                for c in range(TC):
                    act.wait_ge(logit_full, c + 1)
                    act.activation(lt[:, c * TW:(c + 1) * TW], pu[c % 2][0:E, :], ACT.Copy).then_inc(lt_done, 1)
                act.wait_ge(sub_done, 1)
                act.activation(ex[:, :, :], ex[:, :, :], ACT.Exp).then_inc(gate_exp, 1)

                for c in range(TC):
                    for f in range(FT):
                        act.wait_ge(g_full, FT * c + f + 1)
                        if FT * c + f >= 2:
                            act.wait_ge(h_done, FT * c + f - 1)
                        act.activation(sil[f % 2][:, :], pg[f % 2][:, :], ACT.Silu).then_inc(sil_done, 1)

                def turn_x(i, r, first):
                    n = RING * i + r
                    act.wait_ge(xg_turned, n + 1)
                    after(act, up_full, n - 1, first and r < 2)
                    act.activation(xgt[r % 2][:, :, :], py[0][:, 0:D].rearrange("p (k q) -> p k q", k=KC), ACT.Copy)\
                       .then_inc(xgt_done, 1)

                def turn_h(i, r, first):
                    n = RING * i + r
                    act.wait_ge(hg_turned, n + 1)
                    after(act, yg_full, n, first and r == 0)
                    act.activation(hgt[:, :, :], pu[1][:, :].rearrange("p (f q) -> p f q", f=FT), ACT.Copy)\
                       .then_inc(hgt_done, 1)

                def body(i, r, first, last=False):
                    n = RING * i + r
                    begin = first and r == 0
                    act.wait_ge(gate_full, n + 1)
                    after(act, hg_done, n, begin)
                    act.activation(sg[:, :], pg[0][:, :], ACT.Silu).then_inc(sg_done, 1)
                    if not begin:
                        turn_h(*before(i, r), first)
                    if not last:
                        turn_x(*behind(i, r), first and r + 1 < RING)

                turn_x(0, 0, True)
                for r in range(RING):
                    body(0, r, True)
                with act.Fori(1, ROUNDS - 1) as i:
                    for r in range(RING):
                        body(i, r, False)
                for r in range(RING):
                    body(ROUNDS - 1, r, False, r == RING - 1)
                turn_h(ROUNDS - 1, RING - 1, False)

            @block.tensor
            def _(pe):
                for i in range(T):
                    pe.wait_ge(n_done, i + 1)
                    if i >= 4:
                        pe.wait_ge(xnt_done, i - 3)
                    for k in range(KC):
                        mm = pe.transpose(py[i % 4][:, k * P:(k + 1) * P], rows[:, i, k * P:(k + 1) * P],
                                          ident[:, :])
                    mm.then_inc(turned, 1)
                pe.wait_ge(gw_in, 16)
                pe.wait_ge(xnt_done, T)
                for c in range(TC):
                    if c >= 2:
                        pe.wait_ge(lt_done, c - 1)
                    for k in range(KC):
                        mm = pe.matmul(pu[c % 2][0:E, :], gw[:, k, :], xnt[:, k, c * TW:(c + 1) * TW],
                                       start=(k == 0), stop=(k == KC - 1))
                    mm.then_inc(logit_full, 1)
                pe.wait_ge(lt_done, TC)
                for i in range(T):
                    mm = pe.transpose(pg[0][:, i * E:(i + 1) * E], lt[:, i * P:(i + 1) * P], ident[0:E, 0:E])
                mm.then_inc(lt_turned, 1)
                pe.wait_ge(sel_done, 1)
                pe.wait_ge(consts, 5)
                sel_all = sel[:, :, :].rearrange("p t e -> p (t e)")
                pe.matmul(pg[1][:, 0:T * E], below[:, :], sel_all, start=True, stop=True)
                pe.matmul(pg[1][:, T * E:2 * T * E], ones[:, :], sel_all, start=True, stop=True)\
                  .then_inc(count_full, 1)
                pe.wait_ge(wb_in, 32)
                pe.wait_ge(rows_ready, 1)
                for c in range(TC):
                    for f in range(FT):
                        if FT * c + f >= 2:
                            pe.wait_ge(h_done, FT * c + f - 1)
                        for dst, o in ((pg[f % 2], f * P), (pu[f % 2], I + f * P)):
                            for k in range(KC):
                                mm = pe.matmul(dst[:, :], wb[:, k * 2 * I + o:k * 2 * I + o + P],
                                               xnt[:, k, c * TW:(c + 1) * TW], start=(k == 0), stop=(k == KC - 1))
                        mm.then_inc(g_full, 1)
                    pe.wait_ge(h_done, FT * (c + 1))
                    for q in range(4):
                        if c > 0:
                            pe.wait_ge(y_done, 4 * (c - 1) + q + 1)
                        for f in range(FT):
                            mm = pe.matmul(py[q][:, 0:D], h[:, f, q * P:(q + 1) * P],
                                           wb[:, WD + f * D:WD + (f + 1) * D], start=(f == 0), stop=(f == FT - 1))
                        mm.then_inc(y_full, 1)

                pe.wait_ge(wall_in, 32 * E)
                pe.wait_ge(expert_done, 1)
                pe.wait_ge(y_done, T)

                def weights(n):
                    return pe.value_load(expert[0:1, bass.ds(n, 1)], min_val=0, max_val=E - 1)

                def turn_x(i, r, first):
                    n = RING * i + r
                    pe.wait_ge(xg_in[r], 16 * (i + 1))
                    after(pe, xgt_done, n, first and r == 0)
                    for k in range(KC):
                        mm = pe.transpose(py[0][:, k * P:(k + 1) * P], xg[r][:, k * P:(k + 1) * P], ident[:, :])
                    mm.then_inc(xg_turned, 1)

                def turn_h(i, r, first):
                    n = RING * i + r
                    pe.wait_ge(hg_done, n + 1)
                    after(pe, hgt_done, n, first and r == 0)
                    for f in range(FT):
                        mm = pe.transpose(pu[1][:, f * P:(f + 1) * P], hg[:, f * P:(f + 1) * P], ident[:, :])
                    mm.then_inc(hg_turned, 1)

                def down_half(i, r, first):
                    n = RING * i + r
                    w = weights(n)
                    pe.wait_ge(hgt_done, n + 1)
                    after(pe, yg_done, n, first and r == 0)
                    for f in range(FT):
                        mm = pe.matmul(py[1][:, 0:D], hgt[:, f, :], wall[:, bass.ds(w * WE + WD + f * D, D)],
                                       start=(f == 0), stop=(f == FT - 1))
                    mm.then_inc(yg_full, 1)

                def up_half(r, w, dst, o, full):
                    for k in range(KC):
                        mm = pe.matmul(dst[:, :], xgt[r % 2][:, k, :], wall[:, bass.ds(w * WE + k * 2 * I + o, I)],
                                       start=(k == 0), stop=(k == KC - 1))
                    mm.then_inc(full, 1)

                def body(i, r, first, last=False):
                    n = RING * i + r
                    begin = first and r == 0
                    w = weights(n)
                    pe.wait_ge(xgt_done, n + 1)
                    after(pe, sg_done, n, begin)
                    up_half(r, w, pg[0], 0, gate_full)
                    if not begin:
                        turn_h(*before(i, r), first)
                    up_half(r, w, pu[0], I, up_full)
                    if not last:
                        turn_x(*behind(i, r), first and r + 1 < RING)
                    if not begin:
                        down_half(*before(i, r), first)

                turn_x(0, 0, True)
                for r in range(RING):
                    body(0, r, True)
                with pe.Fori(1, ROUNDS - 1) as i:
                    for r in range(RING):
                        body(i, r, False)
                for r in range(RING):
                    body(ROUNDS - 1, r, False, r == RING - 1)
                turn_h(ROUNDS - 1, RING - 1, False)
                down_half(ROUNDS - 1, RING - 1, False)


class Kept:
    pass


def attend(nc, x, ctx_t, w_fc, b_fc, w_q, b_q, w_k, b_k, w_v, b_v, x1, ident):
    with ExitStack() as ctx:
        def sb(name, shape, dt):
            return ctx.enter_context(nc.sbuf_tensor(name, shape, dt))

        t = Kept()
        t.kst = [sb(f"kst{i}", [P, PAIRS, NK], F32R) for i in range(2)]
        t.qst = [sb(f"qst{i}", [P, PAIRS, 2 * NQ], F32R) for i in range(2)]
        t.v = [sb(f"v{i}", [P, KT, VW], F32) for i in range(2)]
        t.whi = sb("whi", [P, 3, KC, D], F32R)
        t.wlo = sb("wlo", [P, 3, KC, D], F32R)
        t.wq = sb("wq", [P, KC, D], F32)
        t.bias = sb("bias", [P, 3, KC], F32)
        t.bias_in = [b_fc, b_q, b_k]
        t.bv = sb("bv", [P, D], F32)
        t.ident = ident
        t.mean = sb("mean", [P, B * QT], F32)
        t.rstd = sb("rstd", [P, B * QT], F32)
        setup(nc, t, x, [w_fc, w_k, w_v], w_q, b_v)
        attention(nc, t, x, ctx_t, x1)


def program(nc, x, ctx_t, w_fc, b_fc, w_q, b_q, w_k, b_k, w_v, b_v, gate_w, gate_up, down, out):
    x1 = nc.dram_tensor("x1", [B, NQ, D], F32).ap()
    with nc.sbuf_tensor("ident", [P, P], F32) as ident:
        attend(nc, x, ctx_t, w_fc, b_fc, w_q, b_q, w_k, b_k, w_v, b_v, x1, ident)
        ffn(nc, ident, x1, gate_w, gate_up, down, out)


def kernel(**inputs):
    import numpy as np
    import concourse.bacc as bacc
    from concourse.bass_utils import run_bass_kernel_spmd

    a = {n: np.asarray(v) for n, v in inputs.items()}
    arrays = {
        "x": a["x"],
        "ctx_t": np.ascontiguousarray(a["ctx_2048"].transpose(0, 2, 1)),
        "w_fc": np.ascontiguousarray(a["L0_xattn_W_fc"].T), "b_fc": a["L0_xattn_b_fc"],
        "w_q": np.ascontiguousarray(a["L0_xattn_W_q"].T), "b_q": a["L0_xattn_b_q"],
        "w_k": np.ascontiguousarray(a["L0_xattn_W_k"].T), "b_k": a["L0_xattn_b_k"],
        "w_v": np.ascontiguousarray(a["L0_xattn_W_v"].reshape(D, D).T), "b_v": a["L0_xattn_b_v"],
        "gate_w": a["L0_ffn_gate_w"],
        "gate_up": np.concatenate([a["L0_ffn_expert_gate_up"], a["L0_ffn_base_gate_up"][None]]),
        "down": np.concatenate([a["L0_ffn_expert_down"], a["L0_ffn_base_down"][None]]),
    }
    nc = bacc.Bacc("TRN2", target_bir_lowering=False, num_devices=1)
    ins = [nc.dram_tensor(n, v.shape, mybir.dt.from_np(v.dtype), kind="ExternalInput").ap()
           for n, v in arrays.items()]
    out = nc.dram_tensor("out", (B, NQ, D), F32, kind="ExternalOutput").ap()
    program(nc, *ins, out)
    r = run_bass_kernel_spmd(nc, [arrays], core_ids=[0])
    return r.results[0]["out"]
```

```python
from contextlib import ExitStack

import concourse.bass as bass
from concourse import mybir

F32 = mybir.dt.float32
F32R = mybir.dt.float32r
I32 = mybir.dt.int32
U32 = mybir.dt.uint32
ALU = mybir.AluOpType
ACT = mybir.ActivationFunctionType
AX = mybir.AxisListType

P = 128
B = 8
NQ = 256
NK = 1601
D = 256
KC = D // P
H = 16
DH = D // H
PAIRS = H // 2
EPS = 1e-5
QT = NQ // P
KT = -(-NK // P)
VS = DH + 1
VW = H * VS + 32 - VS

CHUNKS = [(0, NQ)] + [(o, 256) for o in range(0, NK - 65, 256)] + [(NK - 66, 66)]
NCH = len(CHUNKS)
RANGES = [(0, 402), (402, 400), (802, 400), (NK - 400, 400)]
NEED = [next(c for c in range(1, NCH) if min(CHUNKS[c][0] + CHUNKS[c][1], NK) >= o + w) for o, w in RANGES]
HQ = H * QT
GROUPS = 4
STEPS = GROUPS * KT


CHUNK_RATE = 1.1
MOST = 4
SCORES_FROM = 6
STACK_STEPS = 4
SCORES_END = 3


def side_order():
    chunk = [("turn", 0), ("turn", 1), ("fc", 0), ("proj", 0), ("resid", 0), ("fc", 1)]
    for c in range(2, NCH):
        chunk += [("fc", c), ("proj", c - 1), ("val", c - 1)]
    chunk += [("proj", NCH - 1), ("val", NCH - 1)]
    score = [("score", n) for n in range(len(RANGES) * HQ)]
    steps = [[] for _ in range(STEPS)]
    done, nc_, ns_ = {}, 0, 0
    for s in range(STEPS - SCORES_END):
        if s % KT == 2:
            steps[s].append(("out", (s // KT - 1) % GROUPS))
        while nc_ < len(chunk) and nc_ <= s * CHUNK_RATE:
            steps[s].append(chunk[nc_])
            done[chunk[nc_]] = s
            nc_ += 1
        quota = min(-(-(len(score) - ns_) // (STEPS - SCORES_END - s)), MOST) if s >= SCORES_FROM else 0
        for _ in range(quota):
            ready = done.get(("proj", NEED[min(ns_, len(score) - 1) // HQ]), STEPS) + STACK_STEPS
            if ns_ < len(score) and s >= ready:
                steps[s].append(score[ns_])
                ns_ += 1
    assert nc_ == len(chunk) and ns_ == len(score), (nc_, ns_)
    steps[STEPS - SCORES_END + 1].append(("turnmax", 0))
    return steps


SIDE = side_order()
UNITS = [u for step in SIDE for u in step]
NU = len(UNITS)
UNIT_AT = {u: n for n, u in enumerate(UNITS)}
BEFORE_VALUES = 0.6
BANKS = 3
assert NU % BANKS == 0, NU
FIRST_UNIT = [sum(len(x) for x in SIDE[:s]) for s in range(STEPS + 1)]

STACK_DMAS = {c: 6 if c == 0 else 3 for c in range(NCH)}


def runs(u, phase):
    if phase == "end":
        return u == ("out", GROUPS - 1)
    if phase == "first":
        return u != ("out", GROUPS - 1)
    return phase == "beside" or (u[0] == "out") == (phase == "last")


def units_before(n, phase, bank=None):
    return sum(runs(u, phase) for i, u in enumerate(UNITS[:n]) if bank in (None, i % BANKS))


def units_until(b, n, phase, bank=None):
    count = units_before(n, phase, bank)
    if phase != "alone":
        count += units_before(NU, "alone", bank)
    if phase not in ("alone", "first"):
        count += units_before(NU, "first", bank) + (NU if bank is None else NU // BANKS) * ((B if phase == "end" else b) - 2)
    if phase == "end":
        count += units_before(NU, "last", bank)
    return count


def chunk_lead(c):
    return max(CHUNKS[c - 1][0] + CHUNKS[c - 1][1] - CHUNKS[c][0], 0) if c > 1 else 0


def key_tile(kt):
    k0 = kt * P
    c = min(1 + k0 // 256, NCH - 1)
    return c, k0 - CHUNKS[c][0], min(P, NK - k0)


def layer_statistics(dve, t, x, count, a, b):
    for i in range(a, b):
        op = dve.bn_stats(t.stats[:, i, :], x[:, i - a, :])
        count(op, i == b - 1)
    for i in range(a, b):
        op = dve.bn_aggr(t.mv[:, i, :], t.stats[:, i, :])
        count(op, i == b - 1)


def setup(nc, t, x, weights, w_q, b_v):
    with ExitStack() as tmp:
        wraw = tmp.enter_context(nc.sbuf_tensor("wraw", [P, 3, KC, D], F32))
        xfirst = tmp.enter_context(nc.sbuf_tensor("xfirst", [P, QT, D], F32))
        ones = tmp.enter_context(nc.sbuf_tensor("ones_row", [PAIRS, NK], F32))
        w_in = [tmp.enter_context(nc.semaphore(f"w_in{i}")) for i in range(3)]
        x_first_in = tmp.enter_context(nc.semaphore("x_first_in"))
        small_in = tmp.enter_context(nc.semaphore("small_in"))
        w_hi_done = tmp.enter_context(nc.semaphore("w_hi_done"))
        w_lo_done = tmp.enter_context(nc.semaphore("w_lo_done"))
        stats_done = tmp.enter_context(nc.semaphore("stats_done"))
        var_done = tmp.enter_context(nc.semaphore("var_done"))
        rstd_done = tmp.enter_context(nc.semaphore("rstd_done"))
        set_done = tmp.enter_context(nc.semaphore("set_done"))
        ones_done = tmp.enter_context(nc.semaphore("ones_done"))
        ones_in = tmp.enter_context(nc.semaphore("ones_in"))
        tokens = x.rearrange("b (t p) d -> p (b t) d", p=P)
        with nc.Block() as block:

            @block.sync
            def _(sp):
                sp.dma_start(xfirst[:, :, :], tokens[:, 0:QT, :]).then_inc(x_first_in, 16)
                for i, w in enumerate(weights):
                    sp.dma_start(wraw[:, i, :, :], w.rearrange("(c p) n -> p c n", p=P)).then_inc(w_in[i], 16)
                for i, bias in enumerate(t.bias_in):
                    sp.dma_start(t.bias[:, i, :], bias.rearrange("(c p) -> p c", p=P),
                                 allow_slow_non_contiguous=True).then_inc(small_in, 16)
                sp.dma_start(t.bv[:, :], b_v.partition_broadcast(P)).then_inc(small_in, 16)
                sp.dma_start(t.wq[:, :, :], w_q.rearrange("(c p) n -> p c n", p=P)).then_inc(small_in, 16)
                sp.wait_ge(ones_done, 1)
                for par in range(2):
                    sp.dma_start(t.kst[par][96:97, :, :].rearrange("p a n -> p (a n)").bitcast(F32), ones[:, :])\
                      .then_inc(ones_in, 16)
                sp.dma_start(t.xrest[:, :, :], tokens[:, QT:, :]).then_inc(t.x_rest_in, 16)
                sp.wait_ge(small_in, 16 * (len(t.bias_in) + 2))
                sp.wait_ge(ones_in, 32)

            @block.gpsimd
            def _(pool):
                pool.memset(t.ident[:, :], 0.0).then_inc(set_done, 1)
                pool.memset(t.half[:, :], -0.5).then_inc(set_done, 1)
                pool.wait_ge(set_done, 2)
                pool.affine_select(out=t.ident[:, :], in_=t.ident[:, :], compare_op=ALU.not_equal, fill=1.0,
                                   base=0, pattern=[[-1, P]], channel_multiplier=1).then_inc(set_done, 1)
                for ones_of_v in (t.v_ones, t.v_behind):
                    pool.memset(ones_of_v(0), 1.0).then_inc(set_done, 1)
                pool.wait_ge(var_done, 1)
                pool.tensor_tensor(t.rstd[:, 0:QT], t.vare[:, 0:QT], t.half[:, 0:QT], ALU.pow).then_inc(rstd_done, 1)
                pool.wait_ge(rstd_done, 1)
                pool.wait_ge(set_done, 5)

            @block.vector
            def _(dve):
                dve.memset(ones[:, :], 1.0).then_inc(ones_done, 1)
                dve.memset(t.qst[0][0:96, :, :].bitcast(F32), 0.0).then_inc(ones_done, 1)
                dve.wait_ge(x_first_in, 16)
                done = [0]

                def count(op, wait):
                    done[0] += 1
                    op.then_inc(stats_done, 1)
                    if wait:
                        dve.wait_ge(stats_done, done[0])

                layer_statistics(dve, t, xfirst, count, 0, QT)
                dve.tensor_scalar(t.vare[:, 0:QT], t.mv[:, 0:QT, 1], EPS, None, ALU.add).then_inc(var_done, 1)
                for i in range(3):
                    dve.wait_ge(w_hi_done, i + 1)
                    dve.tensor_tensor(t.wlo[:, i, :, :], wraw[:, i, :, :], t.whi[:, i, :, :].bitcast(F32),
                                      ALU.subtract).then_inc(w_lo_done, 1)
                dve.wait_ge(w_lo_done, 3)
                dve.wait_ge(ones_done, 2)

            @block.scalar
            def _(act):
                for i in range(3):
                    act.wait_ge(w_in[i], 16)
                    act.activation(t.whi[:, i, :, :], wraw[:, i, :, :], ACT.Copy).then_inc(w_hi_done, 1)


def attention(nc, t, x, ctx_t, x1):
    with ExitStack() as ctx:
        def sb(name, shape, dt):
            return ctx.enter_context(nc.sbuf_tensor(name, shape, dt))

        def sem(name):
            return ctx.enter_context(nc.semaphore(name))

        raw = sb("raw", [P, KC, 256], F32)
        chi = sb("chi", [P, KC, 256], F32R)
        clo = sb("clo", [P, KC, 256], F32R)
        fc = sb("fc", [P, KC, 256], F32)
        fhi = sb("fhi", [P, KC, 256], F32R)
        flo = sb("flo", [P, KC, 256], F32R)
        parts = sb("parts", [P, 2, KC, 256], F32R)
        phi, plo = parts[:, 0, :, :], parts[:, 1, :, :]
        parts_at = nc.dram_tensor("parts_at", [NCH, 2, KC, P, 256], F32).ap()
        xn = fc
        res = [sb(f"res{i}", [P, QT, D], F32) for i in range(2)]
        prob = [sb(f"prob{i}", [P, 4 * NQ], F32) for i in range(2)]
        accsb = sb("accsb", [P, NQ], F32)
        att = accsb[:, 0:P].rearrange("p (q j d) -> p q j d", q=QT, d=DH)
        rec = sb("rec", [P, QT, 4], F32)
        mx = sb("mx", [P, HQ, len(RANGES)], F32)
        mxr = sb("mxr", [P, HQ], F32)
        mrow = sb("mrow", [HQ, P], F32R)
        st = [ctx.enter_context(nc.psum_tensor(f"st{i}", [P, 4 * NQ], F32)) for i in range(2)]
        acc = ctx.enter_context(nc.psum_tensor("acc", [P, 512], F32))
        side = [ctx.enter_context(nc.psum_tensor(f"side{i}", [P, 512], F32)) for i in range(BANKS)]

        side_full = sem("side_full")
        side_free = [sem(f"side_free{i}") for i in range(BANKS)]
        raw_in = sem("raw_in")
        x_in = sem("x_in")
        xn_in = sem("xn_in")
        xn_done = sem("xn_done")
        xb_done = sem("xb_done")
        hi_c = sem("hi_c")
        lo_c = sem("lo_c")
        hi_f = sem("hi_f")
        lo_f = sem("lo_f")
        phi_done = sem("phi_done")
        parts_out = sem("parts_out")
        stack_in = [sem(f"stack_in{c}") for c in range(NCH)]
        row_in = sem("row_in")
        mx_done = sem("mx_done")
        st_full = sem("st_full")
        exp_done = sem("exp_done")
        pv_done = sem("pv_done")
        acc_out = sem("acc_out")
        rec_done = sem("rec_done")
        rest_stats = sem("rest_stats")
        rest_var = sem("rest_var")
        rest_rstd = sem("rest_rstd")
        zeroed = sem("zeroed")
        x1_ready = sem("x1_ready")
        x1_out = sem("x1_out")

        def after(eng, s, value, first):
            if not first:
                eng.wait_ge(s, value)

        def unit_full(eng, b, n, phase):
            eng.wait_ge(side_full, units_until(b, n, phase) + 1)

        def unit_out(eng, b, n, phase):
            eng.wait_ge(side_free[n % BANKS], units_until(b, n, phase, n % BANKS) + 1)

        def out_batch(b, g):
            return b - 1 if g < GROUPS - 1 else b - 2

        def pe_unit(pe, b, par, n, phase):
            kind, c = UNITS[n]
            bank = side[n % BANKS]
            after(pe, side_free[n % BANKS], units_until(b, n, phase, n % BANKS), phase == "alone" and
                  units_before(n, phase, n % BANKS) == 0)
            if kind == "turn":
                pe.wait_ge(xn_done, QT * b + QT)
                for q in range(QT):
                    mm = pe.transpose(bank[:, q * P:(q + 1) * P], xn[:, q, c * P:(c + 1) * P], t.ident[:, :])
            elif kind == "resid":
                for q in range(QT):
                    for k in range(KC):
                        mm = pe.transpose(bank[:, q * D + k * P:q * D + (k + 1) * P],
                                          fc[:, k, q * P:(q + 1) * P], t.ident[:, :])
            elif kind == "proj" and c == 0:
                unit_out(pe, b, UNIT_AT["fc", 0], phase)
                for m in range(KC):
                    for k in range(KC):
                        mm = pe.matmul(bank[:, m * 256:m * 256 + NQ], t.wq[:, k, m * P:(m + 1) * P], fc[:, k, :],
                                       start=(k == 0), stop=(k == KC - 1))
            elif kind in ("fc", "proj"):
                w = CHUNKS[c][1]
                if kind == "fc":
                    pe.wait_ge(lo_c, NCH * b + c + 1)
                    wi, hi, lo = 0, chi, clo
                else:
                    pe.wait_ge(lo_f, (NCH - 1) * b + c)
                    wi, hi, lo = 1, fhi, flo
                for m in range(KC):
                    i = 0
                    for k in range(KC):
                        for wt, mov in ((t.whi, hi), (t.whi, lo), (t.wlo, hi)):
                            mm = pe.matmul(bank[:, m * 256:m * 256 + w], wt[:, wi, k, m * P:(m + 1) * P],
                                           mov[:, k, 0:w], start=(i == 0), stop=(i == 3 * KC - 1))
                            i += 1
            elif kind == "val":
                pe.wait_ge(lo_f, (NCH - 1) * b + c)
                tiles = [kt for kt in range(KT) if key_tile(kt)[0] == c]
                for j, kt in enumerate(tiles):
                    _, o, rows = key_tile(kt)
                    i = 0
                    for k in range(KC):
                        for a, wt in ((fhi, t.whi), (fhi, t.wlo), (flo, t.whi)):
                            mm = pe.matmul(bank[0:rows, j * D:(j + 1) * D], a[:, k, o:o + rows],
                                           wt[:, 2, k, :], start=(i == 0), stop=(i == 3 * KC - 1))
                            i += 1
            elif kind == "score":
                r, hq = divmod(c, HQ)
                if hq == 0:
                    o, w = RANGES[r]
                    for i in range(NEED[r - 1] + 1 if r else 0, NEED[r] + 1):
                        pe.wait_ge(stack_in[i], 16 * STACK_DMAS[i] * (b + 1))
                o, w = RANGES[r]
                mm = pe.matmul(bank[:, 0:w], t.qst[par][0:96, hq // 4, (hq % 4) * P:(hq % 4 + 1) * P],
                               t.kst[par][0:96, hq // 4, o:o + w], start=True, stop=True)
            elif kind == "out":
                pe.wait_ge(acc_out, GROUPS * out_batch(b, c) + c + 1)
                for q in range(QT):
                    mm = pe.transpose(bank[:, q * P:(q + 1) * P], accsb[:, q * P:(q + 1) * P], t.ident[:, :])
            else:
                pe.wait_ge(mx_done, b + 1)
                mm = pe.transpose(bank[0:HQ, 0:P], mxr[:, :], t.ident[:, :])
            mm.then_inc(side_full, 1)

        def act_load(act, b, c):
            o, w = CHUNKS[c]
            act.wait_ge(lo_c, NCH * b + c)
            act.dma_start(raw[:, :, 0:w], ctx_t[b].rearrange("(k p) n -> p k n", p=P)[:, :, o:o + w])\
               .then_inc(raw_in, 16)

        def act_chunk_high(act, c):
            w = CHUNKS[c][1]
            act.activation(chi[:, :, 0:w], raw[:, :, 0:w], ACT.Copy).then_inc(hi_c, 1)

        def act_fc_high(act, b, c, phase):
            w = CHUNKS[c][1]
            unit_out(act, b, UNIT_AT["fc", c], phase)
            act.activation(fhi[:, :, 0:w], fc[:, :, 0:w], ACT.Copy).then_inc(hi_f, 1)

        def act_unit(act, b, par, n, phase):
            kind, c = UNITS[n]
            bank, free = side[n % BANKS], side_free[n % BANKS]
            first = phase == "alone"
            if kind in ("resid", "score", "out"):
                return
            unit_full(act, b, n, phase)
            if kind == "turn":
                after(act, lo_c, NCH * b, first)
                act.activation(raw[:, c, :], bank[:, 0:NQ], ACT.Copy).then_inc(free, 1)
                if c == KC - 1:
                    for k in range(KC):
                        unit_out(act, b, UNIT_AT["turn", k], phase)
                    act_chunk_high(act, 0)
                    act_load(act, b, 1)
            elif kind == "fc":
                w = CHUNKS[c][1]
                if c == 1:
                    unit_full(act, b, UNIT_AT["resid", 0], phase)
                else:
                    after(act, lo_f, (NCH - 1) * b + max(c - 1, 0), first and c == 0)
                for m in range(KC):
                    op = act.activation(fc[:, m, 0:w], bank[:, m * 256:m * 256 + w], ACT.Relu,
                                        bias=t.bias[:, 0, m:m + 1])
                op.then_inc(free, 1)
                if c + 1 < NCH:
                    act.wait_ge(raw_in, 16 * ((NCH - 1) * b + c + 1))
                    act_chunk_high(act, c + 1)
                if c == 1:
                    act_fc_high(act, b, 1, phase)
                if c < 2:
                    act_load(act, b, c + 2)
            elif kind == "proj":
                w = CHUNKS[c][1]
                after(act, parts_out, 16 * (NCH * b + c), first and c == 0)
                for m in range(KC):
                    op = act.activation(phi[:, m, 0:w], bank[:, m * 256:m * 256 + w], ACT.Identity,
                                        bias=t.bias[:, 1 if c == 0 else 2, m:m + 1])
                op.then_inc(phi_done, 1)
                if 0 < c < NCH - 3:
                    act_load(act, b, c + 3)
            elif kind == "val":
                tiles = [kt for kt in range(KT) if key_tile(kt)[0] == c]
                rows = key_tile(tiles[0])[2]
                k = len(tiles)
                dst = t.v[par][0:rows, tiles[0]:tiles[0] + k, 0:H * VS].rearrange("p k (h s) -> p k h s", s=VS)
                act.activation(dst[:, :, :, 0:DH],
                               bank[0:rows, 0:k * D].rearrange("p (k h s) -> p k h s", k=k, s=DH),
                               ACT.Copy).then_inc(free, 1)
                if c + 1 < NCH:
                    act_fc_high(act, b, c + 1, phase)
            else:
                after(act, row_in, 16 * b, first)
                act.activation(mrow[:, :], bank[0:HQ, 0:P], ACT.Copy, scale=-1.0).then_inc(free, 1)

        def dve_unit(dve, b, par, n, phase):
            kind, c = UNITS[n]
            bank, free = side[n % BANKS], side_free[n % BANKS]
            if kind == "resid":
                unit_full(dve, b, n, phase)
                dve.wait_ge(xb_done, b + 1)
                dve.tensor_tensor(res[par][:, :, :], bank[:, :].rearrange("p (q d) -> p q d", q=QT),
                                  res[par][:, :, :], ALU.add).then_inc(free, 1)
            elif kind == "proj":
                w = CHUNKS[c][1]
                dve.wait_ge(phi_done, NCH * b + c + 1)
                for m in range(KC):
                    op = dve.scalar_tensor_tensor(plo[:, m, 0:w], in0=bank[:, m * 256:m * 256 + w],
                                                  scalar=t.bias[:, 1 if c == 0 else 2, m:m + 1],
                                                  in1=phi[:, m, 0:w].bitcast(F32), op0=ALU.add, op1=ALU.subtract)
                op.then_inc(free, 1)
            elif kind == "score":
                r, hq = divmod(c, HQ)
                unit_full(dve, b, n, phase)
                dve.tensor_reduce(mx[:, hq, r:r + 1], bank[:, 0:RANGES[r][1]], AX.X, ALU.max)\
                   .then_inc(free, 1)
                if c == len(RANGES) * HQ - 1:
                    unit_out(dve, b, n, phase)
                    for k in range(1, BANKS):
                        unit_out(dve, b, n - k, phase)
                    dve.tensor_reduce(mxr[:, :], mx[:, :, :], AX.X, ALU.max).then_inc(mx_done, 1)
            elif kind == "out":
                dve_normalise(dve, out_batch(b, c), 1 - par if c < GROUPS - 1 else par, b, n, phase)

        def dve_normalise_input(dve, b, par):
            dve.wait_ge(xn_in, 16 * (b + 1))
            for q in range(QT):
                mean, rstd = t.mv[:, bass.ds(QT * b + q, 1), 0], t.rstd[:, bass.ds(QT * b + q, 1)]
                dve.tensor_scalar(xn[:, q, :], xn[:, q, :], mean, rstd, ALU.subtract, ALU.mult).then_inc(xn_done, 1)

        def pool_side(pool, b, par, first):
            def low_chunk(c):
                w = CHUNKS[c][1]
                pool.wait_ge(hi_c, NCH * b + c + 1)
                pool.tensor_tensor(clo[:, :, 0:w], raw[:, :, 0:w], chi[:, :, 0:w].bitcast(F32),
                                   ALU.subtract).then_inc(lo_c, 1)

            def low_fc(c):
                w = CHUNKS[c][1]
                pool.wait_ge(hi_f, (NCH - 1) * b + c)
                pool.tensor_tensor(flo[:, :, 0:w], fc[:, :, 0:w], fhi[:, :, 0:w].bitcast(F32),
                                   ALU.subtract).then_inc(lo_f, 1)

            after(pool, lo_f, (NCH - 1) * b, first)
            pool.dma_start(xn[:, :, :], x[b].rearrange("(t p) d -> p t d", p=P)).then_inc(xn_in, 16)
            low_chunk(0)
            for c in range(NCH):
                if c + 1 < NCH:
                    low_chunk(c + 1)
                if c == 0:
                    pool.wait_ge(x_in, 16 * (b + 1))
                    for q in range(QT):
                        op = pool.tensor_tensor(res[par][:, q, :], res[par][:, q, :], t.bv[:, :], ALU.add)
                    op.then_inc(xb_done, 1)
                if c > 0:
                    low_fc(c)

        def sp_load_x(sp, b, par, first):
            after(sp, x1_out, 16 * (b - 1), first)
            sp.dma_start(res[par][:, :, :], x[b].rearrange("(t p) d -> p t d", p=P)).then_inc(x_in, 16)

        def sp_side(sp, b, par, phase):
            for c in range(NCH):
                sp_stack(sp, b, par, c, phase)
            unit_out(sp, b, UNIT_AT["turnmax", 0], phase)
            sp.dma_start(t.qst[par][96:97, :, :].rearrange("p a n -> p (a n)").bitcast(F32),
                         mrow[:, :].bitcast(F32)).then_inc(row_in, 16)

        def sp_stack(sp, b, par, c, phase):
            w = CHUNKS[c][1]
            at = parts_at[c]
            unit_out(sp, b, UNIT_AT["proj", c], phase)
            sp.dma_start(at[:, :, :, 0:w].rearrange("a k q n -> q (a k) n"),
                         parts[:, :, :, 0:w].rearrange("q a k n -> q (a k) n").bitcast(F32)).then_inc(parts_out, 16)
            sp.wait_ge(parts_out, 16 * (NCH * b + c + 1))
            rows = at.rearrange("a k (p r) n -> a r (k p) n", r=32)
            for g, part in enumerate((0, 0, 1) if c == 0 else (0, 1, 0)):
                if c == 0:
                    for j in range(2):
                        sp.dma_start(t.qst[par][32 * g + 16 * j:32 * g + 16 * j + 16, :, j * NQ:(j + 1) * NQ]
                                     .bitcast(F32), rows[part, 16 * j:16 * j + 16, :, 0:NQ]).then_inc(stack_in[c], 16)
                else:
                    o, lead = CHUNKS[c][0], chunk_lead(c)
                    sp.dma_start(t.kst[par][32 * g:32 * g + 32, :, o + lead:o + w].bitcast(F32),
                                 rows[part, :, :, lead:w]).then_inc(stack_in[c], 16)

        def pe_scores(pe, b, par, s, first):
            g, kt = divmod(s, KT)
            rows = key_tile(kt)[2]
            if s == 0:
                pe.wait_ge(row_in, 16 * (b + 1))
            after(pe, exp_done, STEPS * b + s - 1, first and s < 2)
            for i in range(2):
                mm = pe.matmul(st[s % 2][0:rows, i * 2 * NQ:(i + 1) * 2 * NQ],
                               t.kst[par][0:97, 2 * g + i, kt * P:kt * P + rows],
                               t.qst[par][0:97, 2 * g + i, :], start=True, stop=True)
            mm.then_inc(st_full, 1)

        def pe_values(pe, b, par, s, first):
            g, kt = divmod(s, KT)
            rows = key_tile(kt)[2]
            pe.wait_ge(exp_done, STEPS * b + s + 1)
            if kt == 0:
                after(pe, acc_out, GROUPS * b + g, first and g == 0)
            for j in range(4):
                h = 4 * g + j
                mm = pe.matmul(acc[32 * j:32 * j + 32, 0:NQ], t.v[par][0:rows, kt, VS * h:VS * h + 32],
                               prob[s % 2][0:rows, j * NQ:(j + 1) * NQ], start=(kt == 0), stop=(kt == KT - 1))
            mm.then_inc(pv_done, 1)

        def dve_acc_out(dve, b, g, first):
            dve.wait_ge(pv_done, STEPS * b + KT * (g + 1))
            after(dve, x1_ready, GROUPS * b + g, first and g == 0)
            dve.tensor_copy(accsb[:, :], acc[:, 0:NQ]).then_inc(acc_out, 1)

        def dve_normalise(dve, a, par, b, n, phase):
            g = UNITS[n][1]
            unit_full(dve, b, n, phase)
            o = side[n % BANKS][:, 0:NQ].rearrange("p (q j s) -> p q j s", q=QT, s=32)
            dve.reciprocal(rec[:, :, :], o[:, :, :, DH]).then_inc(rec_done, 1)
            dve.wait_ge(rec_done, GROUPS * a + g + 1)
            dve.tensor_tensor(att, o[:, :, :, 0:DH], rec[:, :, :].unsqueeze(3).broadcast_to([P, QT, 4, DH]),
                              ALU.mult).then_inc(side_free[n % BANKS], 1)
            unit_out(dve, b, n, phase)
            r = res[par][:, :, g * 4 * DH:(g + 1) * 4 * DH]
            dve.tensor_tensor(r, r, att.rearrange("p q j s -> p q (j s)"), ALU.add)\
               .then_inc(x1_ready, 1)

        def sp_store(sp, b, par):
            sp.wait_ge(x1_ready, GROUPS * (b + 1))
            sp.dma_start(x1[b].rearrange("(t p) d -> p t d", p=P), res[par][:, :, :]).then_inc(x1_out, 16)

        def batches(eng, body):
            body(0, 0, True, False)
            with eng.Fori(0, B // 2 - 1) as i:
                body(2 * i + 1, 1, False, False)
                body(2 * i + 2, 0, False, False)
            body(B - 1, 1, False, True)

        def phase_of(first, last):
            return "first" if first else "last" if last else "beside"

        def units_of(s, phase):
            return [n for n in range(FIRST_UNIT[s], FIRST_UNIT[s + 1]) if runs(UNITS[n], phase)]

        ALONE = [n for n in range(NU) if UNITS[n][0] != "out"]

        with nc.Block() as block:

            @block.sync
            def _(sp):
                def body(b, par, first, last):
                    if not first:
                        sp_store(sp, b - 1, 1 - par)
                    if not last:
                        sp_load_x(sp, b + 1, 1 - par, first)
                        sp_side(sp, b + 1, 1 - par, phase_of(first, last))

                sp_load_x(sp, 0, 0, True)
                sp_side(sp, 0, 0, "alone")
                sp.wait_ge(zeroed, 1)
                batches(sp, body)
                sp_store(sp, B - 1, 1)
                sp.wait_ge(x1_out, 16 * B)

            @block.gpsimd
            def _(pool):
                pool_side(pool, 0, 0, True)
                pool.wait_ge(rest_var, 1)
                pool.tensor_tensor(t.rstd[:, QT:], t.vare[:, QT:], t.half[:, QT:], ALU.pow).then_inc(rest_rstd, 1)
                with pool.Fori(0, B // 2 - 1) as i:
                    pool_side(pool, 2 * i + 1, 1, False)
                    pool_side(pool, 2 * i + 2, 0, False)
                pool_side(pool, B - 1, 1, False)

            @block.scalar
            def _(act):
                def body(b, par, first, last):
                    for s in range(STEPS):
                        rows = key_tile(s % KT)[2]
                        act.wait_ge(st_full, STEPS * b + s + 1)
                        after(act, pv_done, STEPS * b + s - 1, first and s < 2)
                        act.activation(prob[s % 2][0:rows, :], st[s % 2][0:rows, :], ACT.Exp,
                                       scale=float(DH) ** -0.5).then_inc(exp_done, 1)
                        for n in units_of(s, phase_of(first, last)):
                            act_unit(act, b + 1, 1 - par, n, phase_of(first, last))

                for n in ALONE:
                    act_unit(act, 0, 0, n, "alone")
                act.wait_ge(zeroed, 3)
                batches(act, body)

            @block.vector
            def _(dve):
                def body(b, par, first, last):
                    if not last:
                        dve_normalise_input(dve, b + 1, 1 - par)
                    for s in range(STEPS):
                        g, kt = divmod(s, KT)
                        if kt == 1 and g > 0:
                            dve_acc_out(dve, b, g - 1, first)
                        for n in units_of(s, phase_of(first, last)):
                            dve_unit(dve, b + 1, 1 - par, n, phase_of(first, last))
                    dve_acc_out(dve, b, GROUPS - 1, first)

                dve_normalise_input(dve, 0, 0)
                dve.wait_ge(t.x_rest_in, 16)
                done = [0]

                def count(op, wait):
                    done[0] += 1
                    op.then_inc(rest_stats, 1)
                    if wait:
                        dve.wait_ge(rest_stats, done[0])

                layer_statistics(dve, t, t.xrest, count, QT, B * QT)
                dve.tensor_scalar(t.vare[:, QT:], t.mv[:, QT:, 1], EPS, None, ALU.add).then_inc(rest_var, 1)
                dve.memset(t.qst[1][0:96, :, :].bitcast(F32), 0.0).then_inc(zeroed, 1)
                for ones_of_v in (t.v_ones, t.v_behind):
                    dve.memset(ones_of_v(1), 1.0).then_inc(zeroed, 1)
                for n in ALONE:
                    dve_unit(dve, 0, 0, n, "alone")
                dve.wait_ge(rest_rstd, 1)
                batches(dve, body)
                dve_unit(dve, B + 1, 1, UNIT_AT["out", GROUPS - 1], "end")

            @block.tensor
            def _(pe):
                def body(b, par, first, last):
                    phase = phase_of(first, last)
                    for s in range(STEPS):
                        pe_scores(pe, b, par, s, first)
                        units = units_of(s, phase)
                        before = round(len(units) * BEFORE_VALUES)
                        for n in units[:before]:
                            pe_unit(pe, b + 1, 1 - par, n, phase)
                        if s > 0:
                            pe_values(pe, b, par, s - 1, first)
                        for n in units[before:]:
                            pe_unit(pe, b + 1, 1 - par, n, phase)
                    pe_values(pe, b, par, STEPS - 1, first)

                for n in ALONE:
                    pe_unit(pe, 0, 0, n, "alone")
                pe.wait_ge(zeroed, 3)
                batches(pe, body)
                pe_unit(pe, B + 1, 1, UNIT_AT["out", GROUPS - 1], "end")


I = 512
E = 8
TOP = 2
FT = I // P
N = B * NQ
T = N // P
TW = 512
TC = N // TW
TQ = TW // P
POOL_TC = 1
SLOT_TILES = -(-(TOP * N // P + E - 1) // 4) * 4
RING = 4
ROUNDS = SLOT_TILES // RING
ROW = D + 2
WE = KC * 2 * I + FT * D
WD = KC * 2 * I


def ffn(nc, ident, x1, gate_w, gate_up, down, out):
    slot_x = nc.dram_tensor("slot_x", [SLOT_TILES * P, ROW], F32).ap()
    part = nc.dram_tensor("part", [TOP * N + SLOT_TILES * P, D], F32).ap()
    with ExitStack() as ctx:
        def sb(name, shape, dt=F32):
            return ctx.enter_context(nc.sbuf_tensor(name, shape, dt))

        def sem(name):
            return ctx.enter_context(nc.semaphore(name))

        def bank(name):
            return ctx.enter_context(nc.psum_tensor(name, [P, 512], F32))

        y = sb("y", [P, T, D])
        rows = sb("rows", [P, T, ROW])
        xnt = sb("xnt", [P, KC, N])
        wall = sb("wall", [P, E * WE])
        wb = sb("wb", [P, WE])
        h = sb("h", [P, FT, TW])
        sil = [sb(f"sil{i}", [P, TW]) for i in range(2)]
        zeros = sb("zeros", [P, D])
        unused = sb("unused", [P, SLOT_TILES, 2])
        gw = sb("gw", [P, KC, E])
        lt = sb("lt", [E, N])
        stats = sb("stats2", [P, T, 6])
        mv = sb("mv2", [P, T, 2])
        vare = sb("vare2", [P, T])
        held = sb("held", [1, SLOT_TILES])
        half = sb("half2", [P, T])
        rstd = sb("rstd2", [P, T])
        top = sb("top", [P, T])
        ex = sb("ex", [P, T, E])
        pr = sb("pr", [P, T, E])
        beats = sb("beats", [P, T, E, E])
        rank = sb("rank", [P, T, E])
        sel = sb("sel", [P, T, E])
        comb = sb("comb", [P, T, E])
        below = sb("below", [P, P])
        ones = sb("ones", [P, P])
        scan = [sb(f"scan{i}", [P, T, E]) for i in range(2)]
        count = sb("count", [P, E])
        iota16 = sb("iota16", [P, T])
        tiles = [sb(f"tiles{i}", [P, E]) for i in range(2)]
        iota40 = sb("iota40", [1, SLOT_TILES])
        ends = sb("ends", [1, SLOT_TILES, E])
        expert_f = sb("expert_f", [1, SLOT_TILES])
        expert = sb("expert", [1, SLOT_TILES], I32)
        slot = sb("slot", [P, T, E])
        pick = sb("pick", [P, T, E])
        slot_f = sb("slot_f", [P, T, TOP])
        slots = sb("slots", [P, T, TOP], U32)
        weight = sb("weight", [P, T, TOP])
        goal = sb("goal", [P, T, TOP], U32)
        xg = [sb(f"xg{i}", [P, ROW]) for i in range(RING)]
        xgt = [sb(f"xgt{i}", [P, KC, P]) for i in range(2)]
        sg = sb("sg", [P, I])
        hg = sb("hg", [P, I])
        hgt = sb("hgt", [P, FT, P])
        yg = [sb(f"yg{i}", [P, D]) for i in range(RING)]
        up_copy, y_copy = [sg, hg], yg[0:2]
        first_part = wall[:, 0:T * D].rearrange("p (t d) -> p t d", d=D)
        second_part = wall[:, T * D:2 * T * D].rearrange("p (t d) -> p t d", d=D)
        pg = [bank(f"pg{i}") for i in range(2)]
        pu = [bank(f"pu{i}") for i in range(2)]
        py = [bank(f"py{i}") for i in range(4)]

        y_in = [sem(f"y_in{c}") for c in range(TC)]
        gw_in = sem("gw_in")
        wb_in = sem("wb_in")
        wall_in = sem("wall_in")
        empty_out = sem("empty_out")
        consts = sem("consts")
        out_done = sem("out_done")
        st_done = sem("st_done")
        v_done = sem("v_done")
        r_done = sem("r_done")
        n_done = sem("n_done")
        turned = sem("turned")
        xnt_done = sem("xnt_done")
        logit_full = sem("logit_full")
        lt_done = sem("lt_done")
        lt_turned = sem("lt_turned")
        chain = sem("chain")
        sub_done = sem("sub_done")
        gate_exp = sem("gate_exp")
        sel_done = sem("sel_done")
        count_full = sem("count_full")
        expert_done = sem("expert_done")
        routed = sem("routed")
        rows_ready = sem("rows_ready")
        rows_out = sem("rows_out")
        g_full = sem("g_full")
        sil_done = sem("sil_done")
        h_done = sem("h_done")
        y_full = sem("y_full")
        up_copied = sem("up_copied")
        y_copied = sem("y_copied")
        y_done = sem("y_done")
        xg_in = [sem(f"xg_in{i}") for i in range(RING)]
        xg_turned = sem("xg_turned")
        xgt_done = sem("xgt_done")
        gate_full = sem("gate_full")
        up_full = sem("up_full")
        sg_done = sem("sg_done")
        hg_done = sem("hg_done")
        hg_turned = sem("hg_turned")
        hgt_done = sem("hgt_done")
        yg_full = sem("yg_full")
        yg_done = sem("yg_done")
        yg_out = [sem(f"yg_out{i}") for i in range(RING)]
        part_in = [sem(f"part_in{c}") for c in range(TC)]
        sum_done = sem("sum_done")

        def after(eng, s, value, first):
            if not first:
                eng.wait_ge(s, value)

        def before(i, r):
            return (i, r - 1) if r else (i - 1, RING - 1)

        def behind(i, r):
            return (i, r + 1) if r + 1 < RING else (i + 1, 0)

        def slot_tiles(eng, body):
            for r in range(RING):
                body(0, r, True)
            with eng.Fori(1, ROUNDS) as i:
                for r in range(RING):
                    body(i, r, False)

        def shared(eng, c):
            for f in range(FT):
                eng.wait_ge(sil_done, FT * c + f + 1)
                if f == 0 and c > 0:
                    eng.wait_ge(y_full, TQ * c)
                up = pu[f % 2]
                if c < POOL_TC:
                    up = up_copy[f % 2]
                    eng.wait_ge(up_copied, FT * c + f + 1)
                eng.tensor_tensor(h[:, f, :], sil[f % 2][:, :], up[:, :], ALU.mult).then_inc(h_done, 1)
            for q in range(TQ):
                i = TQ * c + q
                eng.wait_ge(y_full, i + 1)
                if c == POOL_TC and q == 0:
                    eng.wait_ge(y_done, i)
                part_y = py[q % 2]
                if c < POOL_TC:
                    part_y = y_copy[q % 2]
                    eng.wait_ge(y_copied, i + 1)
                eng.tensor_tensor(y[:, i, :], part_y[:, 0:D], y[:, i, :], ALU.add).then_inc(y_done, 1)

        with nc.Block() as block:

            @block.sync
            def _(sp):
                for c in range(TC):
                    sp.dma_start(y[:, c * TQ:(c + 1) * TQ, :],
                                 x1.rearrange("b (t p) d -> p (b t) d", p=P)[:, c * TQ:(c + 1) * TQ, :])\
                      .then_inc(y_in[c], 16)
                sp.dma_start(gw[:, :, :], gate_w.rearrange("(k p) e -> p k e", p=P)).then_inc(gw_in, 16)
                def load(w, e, s):
                    sp.dma_start(w[:, 0:WD].rearrange("p (k n) -> p k n", k=KC),
                                 gate_up[e].rearrange("(k p) n -> p k n", p=P)).then_inc(s, 16)
                    sp.dma_start(w[:, WD:WE].rearrange("p (k n) -> p k n", k=FT),
                                 down[e].rearrange("(k p) n -> p k n", p=P)).then_inc(s, 16)

                load(wb, E, wb_in)
                sp.wait_ge(consts, 6)
                sp.dma_start(slot_x.rearrange("(t p) r -> p t r", p=P)[:, :, 0:D],
                             zeros[:, :].unsqueeze(1).broadcast_to([P, SLOT_TILES, D])).then_inc(empty_out, 16)
                sp.dma_start(slot_x.rearrange("(t p) r -> p t r", p=P)[:, :, D:ROW], unused[:, :, :])\
                  .then_inc(empty_out, 16)
                for e in range(E):
                    load(wall[:, e * WE:(e + 1) * WE], e, wall_in)
                sp.wait_ge(rows_out, 16 * TOP * T)

                def body(i, r, first):
                    after(sp, yg_out[r], 16 * i, first)
                    sp.dma_start(xg[r][:, :], slot_x[bass.ds((RING * i + r) * P, P), :]).then_inc(xg_in[r], 16)

                slot_tiles(sp, body)
                for r in range(RING):
                    sp.wait_ge(yg_out[r], 16 * ROUNDS)
                for c in range(TC):
                    for a, o in ((first_part, 0), (second_part, N)):
                        sp.dma_start(a[:, c * TQ:(c + 1) * TQ, :],
                                     part[o + c * TW:o + (c + 1) * TW, :].rearrange("(t p) d -> p t d", p=P))\
                          .then_inc(part_in[c], 16)
                for c in range(TC):
                    sp.wait_ge(sum_done, c + 1)
                    sp.dma_start(out.rearrange("b (t p) d -> p (b t) d", p=P)[:, c * TQ:(c + 1) * TQ, :],
                                 y[:, c * TQ:(c + 1) * TQ, :]).then_inc(out_done, 16)
                sp.wait_ge(out_done, 16 * TC)

            @block.gpsimd
            def _(pool):
                pool.memset(half[:, :], -0.5).then_inc(consts, 1)
                pool.memset(ones[:, :], 1.0).then_inc(consts, 1)
                pool.memset(zeros[:, :], 0.0).then_inc(consts, 1)
                pool.memset(unused[:, :, :], 0.0).then_inc(consts, 1)
                pool.wait_ge(consts, 4)
                pool.affine_select(out=below[:, :], in_=ones[:, :], compare_op=ALU.is_gt, fill=0.0,
                                   base=0, pattern=[[1, P]], channel_multiplier=-1).then_inc(consts, 1)
                pool.iota(unused[:, :, 1:2].bitcast(U32), [[P, SLOT_TILES], [1, 1]], base=TOP * N,
                          channel_multiplier=1).then_inc(consts, 1)
                pool.iota(iota16[:, :], [[P, T]], base=0, channel_multiplier=0,
                          allow_small_or_imprecise_dtypes=True).then_inc(consts, 1)
                pool.iota(iota40[:, :], [[1, SLOT_TILES]], base=0, channel_multiplier=0,
                          allow_small_or_imprecise_dtypes=True).then_inc(consts, 1)
                pool.iota(goal[:, :, :], [[P, T], [N, TOP]], base=0, channel_multiplier=1).then_inc(consts, 1)
                for c in range(TC):
                    q = slice(c * TQ, (c + 1) * TQ)
                    pool.wait_ge(v_done, c + 1)
                    pool.tensor_tensor(rstd[:, q], vare[:, q], half[:, q], ALU.pow).then_inc(r_done, 1)
                for c in range(POOL_TC):
                    shared(pool, c)
                pool.wait_ge(empty_out, 32)
                for k in range(TOP):
                    pool.wait_ge(routed, 1)
                    if k > 0:
                        pool.wait_ge(rows_out, 16 * T * k)
                    pool.tensor_copy(rows[:, :, D:D + 1], weight[:, :, k:k + 1]).then_inc(rows_ready, 1)
                    pool.tensor_copy(rows[:, :, D + 1:D + 2].bitcast(U32), goal[:, :, k:k + 1]).then_inc(rows_ready, 1)
                    pool.wait_ge(rows_ready, 2 * k + 2)
                    for i in range(T):
                        pool.indirect_dma_start(
                            out=slot_x, out_offset=bass.IndirectOffsetOnAxis(ap=slots[:, i, k:k + 1], axis=0),
                            in_=rows[:, i, :], in_offset=None).then_inc(rows_out, 16)

                def body(i, r, first):
                    pool.wait_ge(yg_done, RING * i + r + 1)
                    pool.tensor_tensor(held[:, bass.ds(RING * i + r, 1)], half[0:1, 0:1], half[0:1, 0:1], ALU.add)
                    pool.indirect_dma_start(
                        out=part, out_offset=bass.IndirectOffsetOnAxis(ap=xg[r][:, D + 1:D + 2].bitcast(U32), axis=0),
                        in_=yg[r][:, :], in_offset=None).then_inc(yg_out[r], 16)

                slot_tiles(pool, body)

            @block.vector
            def _(dve):
                links = [0]

                def link(op):
                    links[0] += 1
                    op.then_inc(chain, 1)
                    dve.wait_ge(chain, links[0])

                def statistics(c):
                    tiles_of = range(c * TQ, (c + 1) * TQ)
                    dve.wait_ge(y_in[c], 16)
                    for i in tiles_of:
                        dve.bn_stats(stats[:, i, :], y[:, i, :]).then_inc(st_done, 1)
                    dve.wait_ge(st_done, TQ * (2 * c + 1))
                    for i in tiles_of:
                        dve.bn_aggr(mv[:, i, :], stats[:, i, :]).then_inc(st_done, 1)
                    dve.wait_ge(st_done, TQ * (2 * c + 2))
                    dve.tensor_scalar(vare[:, c * TQ:(c + 1) * TQ], mv[:, c * TQ:(c + 1) * TQ, 1], EPS, None, ALU.add)\
                       .then_inc(v_done, 1)

                def normalise(c):
                    dve.wait_ge(r_done, c + 1)
                    for i in range(c * TQ, (c + 1) * TQ):
                        dve.tensor_scalar(rows[:, i, 0:D], y[:, i, :], mv[:, i, 0:1], rstd[:, i:i + 1],
                                          ALU.subtract, ALU.mult).then_inc(n_done, 1)

                for c in range(TC):
                    statistics(c)
                    if c > 0:
                        normalise(c - 1)
                normalise(TC - 1)
                dve.wait_ge(lt_turned, 1)
                logits = py[2][:, 0:T * E].rearrange("p (t e) -> p t e", e=E)

                def by_token(a):
                    return a[:, :].unsqueeze(2).broadcast_to([P, T, E])

                link(dve.tensor_reduce(top[:, :], logits, AX.X, ALU.max))
                dve.tensor_tensor(ex[:, :, :], logits, by_token(top), ALU.subtract).then_inc(sub_done, 1)
                dve.wait_ge(gate_exp, 1)
                link(dve.tensor_reduce(top[:, :], ex[:, :, :], AX.X, ALU.add))
                link(dve.reciprocal(top[:, :], top[:, :]))
                link(dve.tensor_tensor(pr[:, :, :], ex[:, :, :], by_token(top), ALU.mult))
                for e in range(E):
                    if e > 0:
                        dve.tensor_tensor(beats[:, :, e, 0:e], pr[:, :, e:e + 1].broadcast_to([P, T, e]),
                                          pr[:, :, 0:e], ALU.is_gt)
                    op = dve.tensor_tensor(beats[:, :, e, e:E], pr[:, :, e:e + 1].broadcast_to([P, T, E - e]),
                                           pr[:, :, e:E], ALU.is_ge)
                link(op)
                link(dve.tensor_reduce(rank[:, :, :], beats[:, :, :, :].rearrange("p t a b -> p t b a"), AX.X,
                                       ALU.add))
                dve.tensor_scalar(sel[:, :, :], rank[:, :, :], TOP + 0.5, None, ALU.is_lt).then_inc(sel_done, 1)
                dve.wait_ge(sel_done, 1)
                link(dve.tensor_tensor(comb[:, :, :], sel[:, :, :], pr[:, :, :], ALU.mult))
                link(dve.tensor_reduce(top[:, :], comb[:, :, :], AX.X, ALU.add))
                link(dve.reciprocal(top[:, :], top[:, :]))
                link(dve.tensor_tensor(comb[:, :, :], comb[:, :, :], by_token(top), ALU.mult))
                dve.wait_ge(count_full, 1)
                total = py[3][:, T * E:2 * T * E].rearrange("p (t e) -> p t e", e=E)
                within = py[3][:, 0:T * E].rearrange("p (t e) -> p t e", e=E)
                link(dve.tensor_copy(scan[0][:, :, :], total))
                a, step = 0, 1
                while step < T:
                    dve.tensor_copy(scan[1 - a][:, 0:step, :], scan[a][:, 0:step, :])
                    link(dve.tensor_tensor(scan[1 - a][:, step:T, :], scan[a][:, step:T, :],
                                           scan[a][:, 0:T - step, :], ALU.add))
                    a, step = 1 - a, 2 * step
                upto = scan[a]
                link(dve.tensor_copy(count[:, :], upto[:, T - 1, :]))
                link(dve.tensor_tensor(pick[:, :, :], count[:, :].unsqueeze(1).broadcast_to([P, T, E]),
                                       iota16[:, :].unsqueeze(2).broadcast_to([P, T, E]), ALU.is_gt))
                link(dve.tensor_reduce(tiles[0][:, :], pick[:, :, :].rearrange("p t e -> p e t"), AX.X, ALU.add))
                b, step = 0, 1
                while step < E:
                    dve.tensor_copy(tiles[1 - b][:, 0:step], tiles[b][:, 0:step])
                    link(dve.tensor_tensor(tiles[1 - b][:, step:E], tiles[b][:, step:E], tiles[b][:, 0:E - step],
                                           ALU.add))
                    b, step = 1 - b, 2 * step
                ended = tiles[b]
                link(dve.tensor_tensor(ends[:, :, :], iota40[:, :].unsqueeze(2).broadcast_to([1, SLOT_TILES, E]),
                                       ended[0:1, :].unsqueeze(1).broadcast_to([1, SLOT_TILES, E]), ALU.is_ge))
                link(dve.tensor_reduce(expert_f[:, :], ends[:, :, :], AX.X, ALU.add))
                dve.tensor_scalar(expert[:, :], expert_f[:, :], float(E - 1), None, ALU.min).then_inc(expert_done, 1)
                link(dve.tensor_tensor(slot[:, :, :], within, upto[:, :, :], ALU.add))
                link(dve.tensor_tensor(slot[:, :, :], slot[:, :, :], total, ALU.subtract))
                link(dve.scalar_tensor_tensor(slot[:, :, 1:E], in0=ended[:, 0:E - 1].unsqueeze(1)
                                              .broadcast_to([P, T, E - 1]), scalar=float(P),
                                              in1=slot[:, :, 1:E], op0=ALU.mult, op1=ALU.add))
                for k in range(TOP):
                    for src, dst in ((slot, slot_f), (comb, weight)):
                        link(dve.scalar_tensor_tensor(pick[:, :, :], in0=rank[:, :, :], scalar=float(k + 1),
                                                      in1=src[:, :, :], op0=ALU.is_equal, op1=ALU.mult))
                        link(dve.tensor_reduce(dst[:, :, k], pick[:, :, :], AX.X, ALU.add))
                dve.tensor_copy(slots[:, :, :], slot_f[:, :, :]).then_inc(routed, 1)

                for c in range(POOL_TC, TC):
                    if c == POOL_TC:
                        dve.wait_ge(h_done, FT * c)
                    shared(dve, c)

                def scaled(i, r, first):
                    dve.wait_ge(yg_full, RING * i + r + 1)
                    after(dve, yg_out[r], 16 * i, first)
                    dve.tensor_scalar(yg[r][:, :], py[1][:, 0:D], xg[r][:, D:D + 1], None, ALU.mult)\
                       .then_inc(yg_done, 1)

                def body(i, r, first):
                    n = RING * i + r
                    begin = first and r == 0
                    dve.wait_ge(sg_done, n + 1)
                    dve.wait_ge(up_full, n + 1)
                    after(dve, hg_turned, n, begin)
                    dve.tensor_tensor(hg[:, :], sg[:, :], pu[0][:, :], ALU.mult).then_inc(hg_done, 1)
                    if not begin:
                        scaled(*before(i, r), first)

                slot_tiles(dve, body)
                scaled(ROUNDS - 1, RING - 1, False)
                for c in range(TC):
                    q = slice(c * TQ, (c + 1) * TQ)
                    dve.wait_ge(part_in[c], 32)
                    link(dve.tensor_tensor(y[:, q, :], y[:, q, :], first_part[:, q, :], ALU.add))
                    dve.tensor_tensor(y[:, q, :], y[:, q, :], second_part[:, q, :], ALU.add).then_inc(sum_done, 1)

            @block.scalar
            def _(act):
                def copy_rows(c):
                    for i in range(c * TQ, (c + 1) * TQ):
                        act.wait_ge(turned, i + 1)
                        act.activation(xnt[:, :, i * P:(i + 1) * P],
                                       py[i % 2][:, 0:D].rearrange("p (k q) -> p k q", k=KC), ACT.Copy)\
                           .then_inc(xnt_done, 1)

                def copy_logits(c):
                    act.wait_ge(logit_full, c + 1)
                    act.activation(lt[:, c * TW:(c + 1) * TW], py[2 + c % 2][0:E, :], ACT.Copy).then_inc(lt_done, 1)

                for c in range(TC):
                    copy_rows(c)
                    if c > 0:
                        copy_logits(c - 1)
                copy_logits(TC - 1)
                act.wait_ge(sub_done, 1)
                act.activation(ex[:, :, :], ex[:, :, :], ACT.Exp).then_inc(gate_exp, 1)

                for c in range(TC):
                    for f in range(FT):
                        act.wait_ge(g_full, FT * c + f + 1)
                        if FT * c + f >= 2:
                            act.wait_ge(h_done, FT * c + f - 1)
                        act.activation(sil[f % 2][:, :], pg[f % 2][:, :], ACT.Silu).then_inc(sil_done, 1)
                        if c < POOL_TC:
                            act.activation(up_copy[f % 2][:, :], pu[f % 2][:, :], ACT.Copy).then_inc(up_copied, 1)
                    for q in range(TQ if c < POOL_TC else 0):
                        i = TQ * c + q
                        act.wait_ge(y_full, i + 1)
                        if i >= 2:
                            act.wait_ge(y_done, i - 1)
                        act.activation(y_copy[q % 2][:, :], py[q % 2][:, 0:D], ACT.Copy).then_inc(y_copied, 1)

                def turn_x(i, r, first):
                    n = RING * i + r
                    act.wait_ge(xg_turned, n + 1)
                    after(act, up_full, n - 1, first and r < 2)
                    act.activation(xgt[r % 2][:, :, :], py[0][:, 0:D].rearrange("p (k q) -> p k q", k=KC), ACT.Copy)\
                       .then_inc(xgt_done, 1)

                def turn_h(i, r, first):
                    n = RING * i + r
                    act.wait_ge(hg_turned, n + 1)
                    after(act, yg_full, n, first and r == 0)
                    act.activation(hgt[:, :, :], pu[1][:, :].rearrange("p (f q) -> p f q", f=FT), ACT.Copy)\
                       .then_inc(hgt_done, 1)

                def body(i, r, first, last=False):
                    n = RING * i + r
                    begin = first and r == 0
                    act.wait_ge(gate_full, n + 1)
                    after(act, hg_done, n, begin)
                    act.activation(sg[:, :], pg[0][:, :], ACT.Silu).then_inc(sg_done, 1)
                    if not begin:
                        turn_h(*before(i, r), first)
                    if not last:
                        turn_x(*behind(i, r), first and r + 1 < RING)

                turn_x(0, 0, True)
                for r in range(RING):
                    body(0, r, True)
                with act.Fori(1, ROUNDS - 1) as i:
                    for r in range(RING):
                        body(i, r, False)
                for r in range(RING):
                    body(ROUNDS - 1, r, False, r == RING - 1)
                turn_h(ROUNDS - 1, RING - 1, False)

            @block.tensor
            def _(pe):
                def turn_rows(c):
                    for i in range(c * TQ, (c + 1) * TQ):
                        pe.wait_ge(n_done, i + 1)
                        if i >= 2:
                            pe.wait_ge(xnt_done, i - 1)
                        for k in range(KC):
                            mm = pe.transpose(py[i % 2][:, k * P:(k + 1) * P], rows[:, i, k * P:(k + 1) * P],
                                              ident[:, :])
                        mm.then_inc(turned, 1)

                def logits(c):
                    pe.wait_ge(xnt_done, TQ * (c + 1))
                    if c >= 2:
                        pe.wait_ge(lt_done, c - 1)
                    for k in range(KC):
                        mm = pe.matmul(py[2 + c % 2][0:E, :], gw[:, k, :], xnt[:, k, c * TW:(c + 1) * TW],
                                       start=(k == 0), stop=(k == KC - 1))
                    mm.then_inc(logit_full, 1)

                pe.wait_ge(gw_in, 16)
                for c in range(TC):
                    turn_rows(c)
                    if c > 0:
                        logits(c - 1)
                logits(TC - 1)
                pe.wait_ge(lt_done, TC)
                for i in range(T):
                    mm = pe.transpose(py[2][:, i * E:(i + 1) * E], lt[:, i * P:(i + 1) * P], ident[0:E, 0:E])
                mm.then_inc(lt_turned, 1)
                pe.wait_ge(wb_in, 32)
                for c in range(TC):
                    for f in range(FT):
                        if FT * c + f >= 2:
                            pe.wait_ge(h_done, FT * c + f - 1)
                        for dst, o in ((pg[f % 2], f * P), (pu[f % 2], I + f * P)):
                            for k in range(KC):
                                mm = pe.matmul(dst[:, :], wb[:, k * 2 * I + o:k * 2 * I + o + P],
                                               xnt[:, k, c * TW:(c + 1) * TW], start=(k == 0), stop=(k == KC - 1))
                        mm.then_inc(g_full, 1)
                    if c == 0:
                        pe.wait_ge(sel_done, 1)
                        pe.wait_ge(consts, 5)
                        sel_all = sel[:, :, :].rearrange("p t e -> p (t e)")
                        pe.matmul(py[3][:, 0:T * E], below[:, :], sel_all, start=True, stop=True)
                        pe.matmul(py[3][:, T * E:2 * T * E], ones[:, :], sel_all, start=True, stop=True)\
                          .then_inc(count_full, 1)
                    pe.wait_ge(h_done, FT * (c + 1))
                    for q in range(TQ):
                        i = TQ * c + q
                        if i >= 2:
                            pe.wait_ge(y_done, i - 1)
                        for f in range(FT):
                            mm = pe.matmul(py[q % 2][:, 0:D], h[:, f, q * P:(q + 1) * P],
                                           wb[:, WD + f * D:WD + (f + 1) * D], start=(f == 0), stop=(f == FT - 1))
                        mm.then_inc(y_full, 1)

                pe.wait_ge(wall_in, 32 * E)
                pe.wait_ge(expert_done, 1)
                pe.wait_ge(y_done, T)

                def weights(n):
                    return pe.value_load(expert[0:1, bass.ds(n, 1)], min_val=0, max_val=E - 1)

                def turn_x(i, r, first):
                    n = RING * i + r
                    pe.wait_ge(xg_in[r], 16 * (i + 1))
                    after(pe, xgt_done, n, first and r == 0)
                    for k in range(KC):
                        mm = pe.transpose(py[0][:, k * P:(k + 1) * P], xg[r][:, k * P:(k + 1) * P], ident[:, :])
                    mm.then_inc(xg_turned, 1)

                def turn_h(i, r, first):
                    n = RING * i + r
                    pe.wait_ge(hg_done, n + 1)
                    after(pe, hgt_done, n, first and r == 0)
                    for f in range(FT):
                        mm = pe.transpose(pu[1][:, f * P:(f + 1) * P], hg[:, f * P:(f + 1) * P], ident[:, :])
                    mm.then_inc(hg_turned, 1)

                def down_half(i, r, first):
                    n = RING * i + r
                    w = weights(n)
                    pe.wait_ge(hgt_done, n + 1)
                    after(pe, yg_done, n, first and r == 0)
                    for f in range(FT):
                        mm = pe.matmul(py[1][:, 0:D], hgt[:, f, :], wall[:, bass.ds(w * WE + WD + f * D, D)],
                                       start=(f == 0), stop=(f == FT - 1))
                    mm.then_inc(yg_full, 1)

                def up_half(r, w, dst, o, full):
                    for k in range(KC):
                        mm = pe.matmul(dst[:, :], xgt[r % 2][:, k, :], wall[:, bass.ds(w * WE + k * 2 * I + o, I)],
                                       start=(k == 0), stop=(k == KC - 1))
                    mm.then_inc(full, 1)

                def body(i, r, first, last=False):
                    n = RING * i + r
                    begin = first and r == 0
                    w = weights(n)
                    pe.wait_ge(xgt_done, n + 1)
                    after(pe, sg_done, n, begin)
                    up_half(r, w, pg[0], 0, gate_full)
                    if not begin:
                        turn_h(*before(i, r), first)
                    up_half(r, w, pu[0], I, up_full)
                    if not last:
                        turn_x(*behind(i, r), first and r + 1 < RING)
                    if not begin:
                        down_half(*before(i, r), first)

                turn_x(0, 0, True)
                for r in range(RING):
                    body(0, r, True)
                with pe.Fori(1, ROUNDS - 1) as i:
                    for r in range(RING):
                        body(i, r, False)
                for r in range(RING):
                    body(ROUNDS - 1, r, False, r == RING - 1)
                turn_h(ROUNDS - 1, RING - 1, False)
                down_half(ROUNDS - 1, RING - 1, False)


class Kept:
    pass


def attend(nc, x, ctx_t, w_fc, b_fc, w_q, b_q, w_k, b_k, w_v, b_v, x1, ident):
    with ExitStack() as ctx:
        def sb(name, shape, dt):
            return ctx.enter_context(nc.sbuf_tensor(name, shape, dt))

        t = Kept()
        t.kst = [sb(f"kst{i}", [P, PAIRS, NK], F32R) for i in range(2)]
        t.qst = [sb(f"qst{i}", [P, PAIRS, 2 * NQ], F32R) for i in range(2)]
        t.v = [sb(f"v{i}", [P, KT, VW], F32) for i in range(2)]
        t.whi = sb("whi", [P, 3, KC, D], F32R)
        t.wlo = sb("wlo", [P, 3, KC, D], F32R)
        t.wq = sb("wq", [P, KC, D], F32)
        t.bias = sb("bias", [P, 3, KC], F32)
        t.bias_in = [b_fc, b_q, b_k]
        t.bv = sb("bv", [P, D], F32)
        t.ident = ident
        t.stats = sb("stats", [P, B * QT, 6], F32)
        t.mv = sb("mv", [P, B * QT, 2], F32)
        t.vare = sb("vare", [P, B * QT], F32)
        t.half = sb("half", [P, B * QT], F32)
        t.v_ones = lambda par: t.v[par][:, :, 0:H * VS].rearrange("p k (h s) -> p k h s", s=VS)[:, :, :, DH:VS]
        t.v_behind = lambda par: t.v[par][:, :, H * VS:VW]
        t.xrest = t.v[1][:, :, :].rearrange("p k n -> p (k n)")[:, 0:(B - 1) * QT * D]            .rearrange("p (t d) -> p t d", d=D)
        t.x_rest_in = ctx.enter_context(nc.semaphore("x_rest_in"))
        t.rstd = sb("rstd", [P, B * QT], F32)
        setup(nc, t, x, [w_fc, w_k, w_v], w_q, b_v)
        attention(nc, t, x, ctx_t, x1)


def program(nc, x, ctx_t, w_fc, b_fc, w_q, b_q, w_k, b_k, w_v, b_v, gate_w, gate_up, down, out):
    x1 = nc.dram_tensor("x1", [B, NQ, D], F32).ap()
    with nc.sbuf_tensor("ident", [P, P], F32) as ident:
        attend(nc, x, ctx_t, w_fc, b_fc, w_q, b_q, w_k, b_k, w_v, b_v, x1, ident)
        ffn(nc, ident, x1, gate_w, gate_up, down, out)


def kernel(**inputs):
    import numpy as np
    import concourse.bacc as bacc
    from concourse.bass_utils import run_bass_kernel_spmd

    a = {n: np.asarray(v) for n, v in inputs.items()}
    arrays = {
        "x": a["x"],
        "ctx_t": np.ascontiguousarray(a["ctx_2048"].transpose(0, 2, 1)),
        "w_fc": np.ascontiguousarray(a["L0_xattn_W_fc"].T), "b_fc": a["L0_xattn_b_fc"],
        "w_q": np.ascontiguousarray(a["L0_xattn_W_q"].T), "b_q": a["L0_xattn_b_q"],
        "w_k": np.ascontiguousarray(a["L0_xattn_W_k"].T), "b_k": a["L0_xattn_b_k"],
        "w_v": np.ascontiguousarray(a["L0_xattn_W_v"].reshape(D, D).T), "b_v": a["L0_xattn_b_v"],
        "gate_w": a["L0_ffn_gate_w"],
        "gate_up": np.concatenate([a["L0_ffn_expert_gate_up"], a["L0_ffn_base_gate_up"][None]]),
        "down": np.concatenate([a["L0_ffn_expert_down"], a["L0_ffn_base_down"][None]]),
    }
    nc = bacc.Bacc("TRN2", target_bir_lowering=False, num_devices=1)
    ins = [nc.dram_tensor(n, v.shape, mybir.dt.from_np(v.dtype), kind="ExternalInput").ap()
           for n, v in arrays.items()]
    out = nc.dram_tensor("out", (B, NQ, D), F32, kind="ExternalOutput").ap()
    program(nc, *ins, out)
    r = run_bass_kernel_spmd(nc, [arrays], core_ids=[0])
    return r.results[0]["out"]
```
